# Optimizing a Trainium2 kernel written in Bass

```python
import numpy as np
import jax
import jax.numpy as jnp

def _softmax(x, axis=-1):
    return jax.nn.softmax(x, axis=axis)

def _gelu(x):
    return jax.nn.gelu(x, approximate=True)

def _silu(x):
    return jax.nn.silu(x)

def _sigmoid(x):
    return jax.nn.sigmoid(x)

def _layernorm(x, axis=-1, eps=1e-05):
    m = jnp.mean(x, axis=axis, keepdims=True)
    v = jnp.var(x, axis=axis, keepdims=True)
    return (x - m) / jnp.sqrt(v + eps)

def _scatter_add(tgt, idx, src, axis=0):
    return tgt.at[idx].add(src)

def _segment_sum(src, seg, n):
    return jax.ops.segment_sum(src, seg, n)
kernel_name = 'mk_adaln_d2_jaxref_r8_0ebbdf'

def setup_inputs(seed: int=0):
    np.random.seed(seed)
    _w = jnp.asarray

    def _L0_attn_setup():
        import jax, jax.numpy as jnp
        import numpy as np
        DIM = 128
        HEADS = 16
        HEAD_DIM = DIM // HEADS
        SCALE = DIM ** (-0.5)
        key = jax.random.key(seed)
        k1, k2, k3, k4 = jax.random.split(key, 4)
        B, N = (4, 256)
        x = jax.random.normal(k1, (B, N, DIM), dtype=jnp.float32)
        w_qkv = jax.random.normal(k2, (3 * DIM, DIM), dtype=jnp.float32) * DIM ** (-0.5)
        w_out = jax.random.normal(k3, (DIM, DIM), dtype=jnp.float32) * DIM ** (-0.5)
        b_out = jax.random.normal(k4, (DIM,), dtype=jnp.float32) * 0.01
        return {'x': x, 'w_qkv': w_qkv, 'w_out': w_out, 'b_out': b_out}
    _L0_attn_in = _L0_attn_setup()

    def _L0_ffn_setup():
        import jax, jax.numpy as jnp
        import numpy as np
        DIM = 128
        HIDDEN = 512
        E = 8
        K = 2

        def _ffn_hidden(h, multiple_of=32):
            h = int(2 * h / 3)
            return multiple_of * ((h + multiple_of - 1) // multiple_of)
        EXP_HID = _ffn_hidden(HIDDEN)
        SH_HID = _ffn_hidden(HIDDEN // 2)

        def _swiglu(t, a, b, c):
            return jax.nn.silu(t @ a) * (t @ c) @ b
        key = jax.random.key(seed)
        ks = jax.random.split(key, 8)

        def xavier(k, shape, fan_in, fan_out):
            lim = np.sqrt(6.0 / (fan_in + fan_out)).astype(np.float32)
            return jax.random.uniform(k, shape, jnp.float32, -lim, lim)
        return {'x': jax.random.normal(ks[0], (2, 256, DIM), jnp.float32), 'gate_w': xavier(ks[1], (E, DIM), DIM, E), 'w1': xavier(ks[2], (E, DIM, EXP_HID), DIM, EXP_HID), 'w2': xavier(ks[3], (E, EXP_HID, DIM), EXP_HID, DIM), 'w3': xavier(ks[4], (E, DIM, EXP_HID), DIM, EXP_HID), 'sw1': xavier(ks[5], (DIM, SH_HID), DIM, SH_HID), 'sw2': xavier(ks[6], (SH_HID, DIM), SH_HID, DIM), 'sw3': xavier(ks[7], (DIM, SH_HID), DIM, SH_HID)}
    _L0_ffn_in = _L0_ffn_setup()
    _L0_c = _w((lambda *s: np.random.randn(*s).astype(np.float32) * 0.05)(8, 128))
    _L0_wmod = _w((lambda *s: np.random.randn(*s).astype(np.float32) * 0.05)(128, 6 * 128) * 128 ** (-0.5))

    def _L1_attn_setup():
        import jax, jax.numpy as jnp
        import numpy as np
        B, T, C = (2, 256, 128)
        LAT = 32
        N_HEAD = 16
        HEAD_DIM = C // N_HEAD
        SCALE = 1.0 / np.sqrt(HEAD_DIM).astype(np.float32)
        key = jax.random.key(seed)
        ks = jax.random.split(key, 9)
        s_in = 0.02
        return {'x': jax.random.normal(ks[0], (B, T, C), dtype=jnp.float32), 'wq_lat': jax.random.normal(ks[1], (C, LAT), dtype=jnp.float32) * s_in, 'wk_lat': jax.random.normal(ks[2], (C, LAT), dtype=jnp.float32) * s_in, 'wv_lat': jax.random.normal(ks[3], (C, LAT), dtype=jnp.float32) * s_in, 'wq_heads': jax.random.normal(ks[4], (LAT, C), dtype=jnp.float32) * s_in, 'wk_heads': jax.random.normal(ks[5], (LAT, C), dtype=jnp.float32) * s_in, 'wv_heads': jax.random.normal(ks[6], (LAT, C), dtype=jnp.float32) * s_in, 'w_proj': jax.random.normal(ks[7], (C, C), dtype=jnp.float32) * s_in, 'b_proj': jnp.zeros((C,), dtype=jnp.float32)}
    _L1_attn_in = _L1_attn_setup()

    def _L1_ffn_setup():
        import jax, jax.numpy as jnp
        import numpy as np
        NUM_EXPERTS = 8
        TOP_K = 2
        D_MODEL = 128
        D_FF = 1 * D_MODEL
        B, T = (4, 256)
        key = jax.random.key(seed)
        k_x, k_r, k_w1, k_w2 = jax.random.split(key, 4)
        x = jax.random.normal(k_x, (B, T, D_MODEL), dtype=jnp.float32)
        Wr = jax.random.normal(k_r, (D_MODEL, NUM_EXPERTS), dtype=jnp.float32) * 0.02
        W1 = jax.random.normal(k_w1, (NUM_EXPERTS, D_MODEL, D_FF), dtype=jnp.float32) * 0.02
        W2 = jax.random.normal(k_w2, (NUM_EXPERTS, D_FF, D_MODEL), dtype=jnp.float32) * 0.02
        return {'x': x, 'Wr': Wr, 'W1': W1, 'W2': W2}
    _L1_ffn_in = _L1_ffn_setup()
    _L1_c = _w((lambda *s: np.random.randn(*s).astype(np.float32) * 0.05)(8, 128))
    _L1_wmod = _w((lambda *s: np.random.randn(*s).astype(np.float32) * 0.05)(128, 6 * 128) * 128 ** (-0.5))
    _d = {'L0_attn_x': _L0_attn_in['x'], 'L0_attn_w_qkv': _L0_attn_in['w_qkv'], 'L0_attn_w_out': _L0_attn_in['w_out'], 'L0_attn_b_out': _L0_attn_in['b_out'], 'L0_ffn_gate_w': _L0_ffn_in['gate_w'], 'L0_ffn_w1': _L0_ffn_in['w1'], 'L0_ffn_w2': _L0_ffn_in['w2'], 'L0_ffn_w3': _L0_ffn_in['w3'], 'L0_ffn_sw1': _L0_ffn_in['sw1'], 'L0_ffn_sw2': _L0_ffn_in['sw2'], 'L0_ffn_sw3': _L0_ffn_in['sw3'], 'L0_c': _L0_c, 'L0_wmod': _L0_wmod, 'L1_attn_wq_lat': _L1_attn_in['wq_lat'], 'L1_attn_wk_lat': _L1_attn_in['wk_lat'], 'L1_attn_wv_lat': _L1_attn_in['wv_lat'], 'L1_attn_wq_heads': _L1_attn_in['wq_heads'], 'L1_attn_wk_heads': _L1_attn_in['wk_heads'], 'L1_attn_wv_heads': _L1_attn_in['wv_heads'], 'L1_attn_w_proj': _L1_attn_in['w_proj'], 'L1_attn_b_proj': _L1_attn_in['b_proj'], 'L1_ffn_Wr': _L1_ffn_in['Wr'], 'L1_ffn_W1': _L1_ffn_in['W1'], 'L1_ffn_W2': _L1_ffn_in['W2'], 'L1_c': _L1_c, 'L1_wmod': _L1_wmod}
    _x0 = _d['L0_attn_x']
    _d['L0_attn_x'] = jax.random.normal(jax.random.fold_in(jax.random.key(seed), 1), (8, 512, 128), dtype=_x0.dtype)
    del _x0
    return _d

def reference(L0_attn_x, L0_attn_w_qkv, L0_attn_w_out, L0_attn_b_out, L0_ffn_gate_w, L0_ffn_w1, L0_ffn_w2, L0_ffn_w3, L0_ffn_sw1, L0_ffn_sw2, L0_ffn_sw3, L0_c, L0_wmod, L1_attn_wq_lat, L1_attn_wk_lat, L1_attn_wv_lat, L1_attn_wq_heads, L1_attn_wk_heads, L1_attn_wv_heads, L1_attn_w_proj, L1_attn_b_proj, L1_ffn_Wr, L1_ffn_W1, L1_ffn_W2, L1_c, L1_wmod):

    def _L0_attn_ref(x, w_qkv, w_out, b_out):
        import jax, jax.numpy as jnp
        import numpy as np
        DIM = 128
        HEADS = 16
        HEAD_DIM = DIM // HEADS
        SCALE = DIM ** (-0.5)
        b, n, _ = x.shape
        qkv = jnp.einsum('bnd,ed->bne', x, w_qkv)
        qkv = qkv.reshape(b, n, 3, HEADS, HEAD_DIM)
        q, k, v = (qkv[:, :, i].transpose(0, 2, 1, 3) for i in range(3))
        dots = jnp.einsum('bhid,bhjd->bhij', q, k) * SCALE
        attn = jax.nn.softmax(dots, axis=-1)
        out = jnp.einsum('bhij,bhjd->bhid', attn, v)
        out = out.transpose(0, 2, 1, 3).reshape(b, n, HEADS * HEAD_DIM)
        return jnp.einsum('bnd,ed->bne', out, w_out) + b_out

    def _L0_ffn_ref(x, gate_w, w1, w2, w3, sw1, sw2, sw3):
        import jax, jax.numpy as jnp
        import numpy as np
        DIM = 128
        HIDDEN = 512
        E = 8
        K = 2

        def _ffn_hidden(h, multiple_of=32):
            h = int(2 * h / 3)
            return multiple_of * ((h + multiple_of - 1) // multiple_of)
        EXP_HID = _ffn_hidden(HIDDEN)
        SH_HID = _ffn_hidden(HIDDEN // 2)

        def _swiglu(t, a, b, c):
            return jax.nn.silu(t @ a) * (t @ c) @ b
        B, S, D = x.shape
        xt = x.reshape(-1, D)
        T = xt.shape[0]
        logits = xt @ gate_w.T
        scores = jax.nn.softmax(logits, axis=-1)
        topk_w, topk_i = jax.lax.top_k(scores, K)
        comb = jnp.zeros((T, E), x.dtype).at[jnp.arange(T)[:, None], topk_i].add(topk_w)
        y = jnp.zeros_like(xt)
        for e in range(E):
            y = y + comb[:, e:e + 1] * _swiglu(xt, w1[e], w2[e], w3[e])
        y = y.reshape(B, S, D)
        return y + _swiglu(x, sw1, sw2, sw3)

    def _L1_attn_ref(x, wq_lat, wk_lat, wv_lat, wq_heads, wk_heads, wv_heads, w_proj, b_proj):
        import jax, jax.numpy as jnp
        import numpy as np
        B, T, C = (2, 256, 128)
        LAT = 32
        N_HEAD = 16
        HEAD_DIM = C // N_HEAD
        SCALE = 1.0 / np.sqrt(HEAD_DIM).astype(np.float32)
        Bx, Tx, Cx = x.shape
        q = x @ wq_lat @ wq_heads
        k = x @ wk_lat @ wk_heads
        v = x @ wv_lat @ wv_heads
        q = q.reshape(Bx, Tx, N_HEAD, HEAD_DIM).transpose(0, 2, 1, 3)
        k = k.reshape(Bx, Tx, N_HEAD, HEAD_DIM).transpose(0, 2, 1, 3)
        v = v.reshape(Bx, Tx, N_HEAD, HEAD_DIM).transpose(0, 2, 1, 3)
        att = jnp.einsum('bhqd,bhkd->bhqk', q, k) * SCALE
        causal = jnp.tril(jnp.ones((Tx, Tx), dtype=bool))
        att = jnp.where(causal[None, None], att, -jnp.inf)
        att = jax.nn.softmax(att, axis=-1)
        y = jnp.einsum('bhqk,bhkd->bhqd', att, v)
        y = y.transpose(0, 2, 1, 3).reshape(Bx, Tx, Cx)
        return y @ w_proj + b_proj

    def _L1_ffn_ref(x, Wr, W1, W2):
        import jax, jax.numpy as jnp
        import numpy as np
        NUM_EXPERTS = 8
        TOP_K = 2
        D_MODEL = 128
        D_FF = 1 * D_MODEL
        B, T = (4, 256)
        Bq, Tq, C = x.shape
        xf = x.reshape(-1, C)
        N = xf.shape[0]
        E = W1.shape[0]
        probs = jax.nn.softmax(xf @ Wr, axis=-1)
        w, idx = jax.lax.top_k(probs, TOP_K)
        comb = jnp.zeros((N, E), xf.dtype).at[jnp.arange(N)[:, None], idx].add(w)
        mid = jnp.einsum('nd,edf->enf', xf, W1)
        mid = jnp.square(jnp.maximum(mid, 0.0))
        y = jnp.einsum('enf,efd->end', mid, W2)
        out = jnp.einsum('end,ne->nd', y, comb)
        return out.reshape(Bq, Tq, C)
    x = L0_attn_x
    mod = (_silu(L0_c) @ L0_wmod).reshape(L0_c.shape[0], 6, 1, -1)
    sa, ca, ga, sb, cb, gb = (mod[:, 0], mod[:, 1], mod[:, 2], mod[:, 3], mod[:, 4], mod[:, 5])
    ga = (2 * (ga >= 0) - 1) * jnp.maximum(jnp.abs(ga), 0.25)
    gb = (2 * (gb >= 0) - 1) * jnp.maximum(jnp.abs(gb), 0.25)
    h = _layernorm(x, axis=-1) * (1 + ca) + sa
    x = x + ga * _L0_attn_ref(h, L0_attn_w_qkv, L0_attn_w_out, L0_attn_b_out)
    h = _layernorm(x, axis=-1) * (1 + cb) + sb
    x = x + gb * _L0_ffn_ref(h, L0_ffn_gate_w, L0_ffn_w1, L0_ffn_w2, L0_ffn_w3, L0_ffn_sw1, L0_ffn_sw2, L0_ffn_sw3)
    mod = (_silu(L1_c) @ L1_wmod).reshape(L1_c.shape[0], 6, 1, -1)
    sa, ca, ga, sb, cb, gb = (mod[:, 0], mod[:, 1], mod[:, 2], mod[:, 3], mod[:, 4], mod[:, 5])
    ga = (2 * (ga >= 0) - 1) * jnp.maximum(jnp.abs(ga), 0.25)
    gb = (2 * (gb >= 0) - 1) * jnp.maximum(jnp.abs(gb), 0.25)
    h = _layernorm(x, axis=-1) * (1 + ca) + sa
    x = x + ga * _L1_attn_ref(h, L1_attn_wq_lat, L1_attn_wk_lat, L1_attn_wv_lat, L1_attn_wq_heads, L1_attn_wk_heads, L1_attn_wv_heads, L1_attn_w_proj, L1_attn_b_proj)
    h = _layernorm(x, axis=-1) * (1 + cb) + sb
    x = x + gb * _L1_ffn_ref(h, L1_ffn_Wr, L1_ffn_W1, L1_ffn_W2)
    return x

_drawn_inputs = setup_inputs


def setup_inputs(seed=0):
    import zlib

    import numpy as np

    out = dict(_drawn_inputs(seed))
    spreads = {'L1_attn_b_proj': (0.0, 0.338)}
    factors = {'L0_attn_w_qkv': 3.751,
     'L0_attn_w_out': 3.277,
     'L0_attn_b_out': 8.0,
     'L1_attn_wq_lat': 8.0,
     'L1_attn_wk_lat': 8.0,
     'L1_attn_wv_lat': 8.0,
     'L1_attn_wq_heads': 8.0,
     'L1_attn_wk_heads': 8.0,
     'L1_attn_wv_heads': 8.0,
     'L1_attn_w_proj': 8.0,
     'L1_ffn_Wr': 8.0,
     'L1_ffn_W1': 8.0,
     'L1_ffn_W2': 8.0}
    for name, (base, spread) in spreads.items():
        noise = np.random.default_rng([zlib.crc32(name.encode()), seed]).standard_normal(out[name].shape)
        drawn = base * np.exp(spread * noise) if base else spread * noise
        out[name] = jnp.asarray(drawn.astype(out[name].dtype))
    for name, factor in factors.items():
        out[name] = (out[name] * factor).astype(out[name].dtype)
    return out
```

```python
from contextlib import ExitStack

import numpy as np
import concourse.bass as bass
from concourse import mybir

F32 = mybir.dt.float32
BF16 = mybir.dt.bfloat16
U32 = mybir.dt.uint32
ALU = mybir.AluOpType
ACT = mybir.ActivationFunctionType
AX = mybir.AxisListType

NB, S, D = 8, 512, 128
NT = S // 128
H, DH = 16, 8
E = 8
NPROD = 9
KA, KB = 96, 128
BIG = -float(2.0 ** 126)
SC0 = float(128 ** (-0.5))
SC1 = float(1.0 / np.sqrt(8).astype(np.float32))
EPS = 1e-5
ONES = float(np.array([0x3F803F80], np.uint32).view(np.float32)[0])

W0 = {"q": 0, "k": 128, "v": 256, "o": 384, "g": 512}
W0N = 520
W1 = {"lat": 0, "q": 128, "k": 256, "v": 384, "o": 512, "g": 640}
W1N = 648


class Mark:

    def __init__(self, sem, value):
        self.sem, self.value = sem, value


class Queues:

    def __init__(self):
        self.count = {}
        self.stream = None

    def open(self):
        self.stream = []

    def seg(self, weight):
        self.stream.append((weight, []))

    def put(self, engine, waits, fn, sem=None, by=1):
        self.stream[-1][1].append((engine, [w for w in waits if w is not None], fn, sem, by))
        if sem is None:
            return None
        self.count[sem] = self.count.get(sem, 0) + by
        return Mark(sem, self.count[sem])

    def dma(self, engine, waits, out, in_, sem):
        return self.put(engine, waits, lambda e: e.dma_start(out, in_), sem, 16)


class Bank:

    def __init__(self, ap):
        self.ap, self.free = ap, []


class Ring:
    def __init__(self, items):
        self.items, self.n = items, 0

    def next(self):
        self.n += 1
        return self.items[(self.n - 1) % len(self.items)]


def merge(parts):
    keyed = []
    for k, (stream, a, b) in enumerate(parts):
        total = sum(w for w, _ in stream) or 1.0
        at = 0.0
        for n, (w, ins) in enumerate(stream):
            keyed.append((a + (b - a) * at / total, k, n, ins))
            at += w
    keyed.sort(key=lambda x: x[:3])
    return [i for x in keyed for i in x[3]]


def program(nc, xin, cT, wm, w0, wf1, wf3, wf2, w1, wr1, wr2, bo, out):
    ctx = ExitStack()
    with ctx:
        def sb(name, shape, dt=F32):
            return ctx.enter_context(nc.sbuf_tensor(name, shape, dt))

        def ps(name, shape, dt=F32):
            return ctx.enter_context(nc.psum_tensor(name, shape, dt))

        def dram(name, shape, dt=F32):
            return nc.dram_tensor(name, shape, dt, kind="Internal").ap()

        X = sb("X", [128, NB * NT, D])
        w0s = sb("w0s", [128, W0N])
        w1s = sb("w1s", [128, W1N])
        f1 = sb("f1", [128, 8 * 352 + 256])
        f3 = sb("f3", [128, 8 * 352 + 256])
        f2 = sb("f2", [128, E * 3 + 2, 128])
        r1 = f1[:, 0:1024].rearrange("p (e f) -> p e f", e=E)
        r2 = f1[:, 1024:2048].rearrange("p (e f) -> p e f", e=E)
        cs = sb("cs", [128, 3, NB])
        mods = sb("mods", [128, 2, 6, NB])
        gat = sb("gat", [NB, 4, 2, 128])
        bos = sb("bos", [128, 2, 128])
        ident = sb("ident", [128, 128])
        identb = sb("identb", [128, 128], BF16)
        maskq = sb("maskq", [128, 128], BF16)
        maskk = sb("maskk", [128, 128], BF16)
        iota8 = sb("iota8", [128, E])
        half = sb("half", [128, NT])
        QS = [sb(f"QS{i}", [128, H, S], BF16) for i in range(2)]
        KS = [sb(f"KS{i}", [128, H, S], BF16) for i in range(2)]
        VS = [sb(f"VS{i}", [128, NT, H, 16]) for i in range(3)]
        NE_ = 8
        ES = [sb(f"ES{i}", [128, S]) for i in range(NE_)]
        US = [sb(f"US{i}", [128, S]) for i in range(2)]
        OT = sb("OT", [128, S])
        DR = sb("DR", [128, S])
        DC = sb("DC", [128, 2, 64])
        nm = sb("nm", [128, 64])
        nmp = sb("nmp", [64, 3, 128], BF16)
        nmr = sb("nmr", [64, 128])
        st6 = sb("st6", [128, 2, NT, 6])
        mv = sb("mv", [128, 2, NT, 2])
        rs = sb("rs", [128, 2, 2, NT])
        ya = sb("ya", [128, NT, 128])
        lat = sb("lat", [128, S])
        xn = [lat[:, :].rearrange("p (t f) -> p t f", t=NT), ya[:, :, :]]
        hT = [sb(f"hT{i}", [128, S]) for i in range(2)]
        sp = [sb(f"sp{i}", [128, 3, S], BF16) for i in range(2)]
        sr = sb("sr", [128, S])
        GT = [sb(f"GT{i}", [128, 2, 128]) for i in range(4)]
        lg = sb("lg", [128, 6, NT, E])
        m8 = sb("m8", [128, NT, 8])
        i8 = sb("i8", [128, NT, 8], U32)
        if8 = sb("if8", [128, NT, 8])
        sm = sb("sm", [128, 3, NT])
        tt = [sb(f"tt{i}", [128, S]) for i in range(2)]
        NHD = 4
        hd = [sb(f"hd{i}", [128, S]) for i in range(NHD)]
        wms = [hd[0], hd[1]]
        yt = [sb(f"yt{i}", [128, NT, 128]) for i in range(2)]
        pt = yt[0]

        banks = [Bank(ps(f"ps{i}", [128, 512])) for i in range(8)]

        d_q = [dram(f"d_q{i}", [3, DH, H * S], BF16) for i in range(2)]
        d_k = [dram(f"d_k{i}", [3, DH, H * S], BF16) for i in range(2)]
        d_m = [dram(f"d_m{i}", [3, 64, 128], BF16) for i in range(2)]
        d_u = [dram(f"d_u{i}", [4, 4, 16, S]) for i in range(2)]
        d_r = [dram(f"d_r{i}", [H, S]) for i in range(2)]
        d_g = dram("d_g", [2, NB, 2, 128])

        q = Queues()
        put, dma, seg = q.put, q.dma, q.seg

        last = {}

        q.open()
        seg(0)
        l_c = dma("sp", [], cs[:, 2, :], cT[0], "l_c0")
        xv = xin.rearrange("b (t p) d -> p (b t) d", p=128)
        for b in range(NB):
            last["x", b] = dma("sp", [], X[:, NT * b:NT * b + NT, :], xv[:, NT * b:NT * b + NT, :], f"l_x{b}")
            if b == 0:
                l_w0 = dma("sp", [], w0s[:, :], w0, "l_w0")
                l_wm = [dma("act", [], wms[n][:, 0:384], wm[0, :, 384 * n:384 * n + 384], f"l_wm0{n}") for n in range(2)]
        l_bo = dma("sp", [], bos[:, :, :], bo.partition_broadcast(128), "l_bo")
        l_f1 = dma("act", [], f1[:, :], wf1, "l_f1")
        l_f3 = dma("act", [], f3[:, :], wf3, "l_f3")
        l_f2 = dma("act", [], f2[:, :, :], wf2, "l_f2")
        l_w1 = dma("act", [], w1s[:, :], w1, "l_w1")

        z = put("pool", [], lambda e: e.memset(ident[:, :], 0.0), "c_id")
        z1 = put("pool", [], lambda e: e.memset(maskq[:, :], 0.0), "c_id")
        z2 = put("pool", [], lambda e: e.memset(maskk[:, :], 0.0), "c_id")
        c_id = put("pool", [z], lambda e: e.affine_select(
            out=ident[:, :], in_=ident[:, :], compare_op=ALU.not_equal, fill=1.0, base=0,
            pattern=[[-1, 128]], channel_multiplier=1), "c_id")
        c_mq = put("pool", [z1], lambda e: e.affine_select(
            out=maskq[:, :], in_=maskq[:, :], compare_op=ALU.is_ge, fill=BIG, base=0,
            pattern=[[-1, 128]], channel_multiplier=1), "c_id")
        c_mk = put("pool", [z2], lambda e: e.affine_select(
            out=maskk[:, :], in_=maskk[:, :], compare_op=ALU.is_ge, fill=BIG, base=0,
            pattern=[[1, 128]], channel_multiplier=-1), "c_id")
        c_io = put("pool", [], lambda e: e.iota(iota8[:, :], [[1, E]], base=0, channel_multiplier=0,
                                                allow_small_or_imprecise_dtypes=True), "c_id")
        c_hf = put("pool", [], lambda e: e.memset(half[:, :], -0.5), "c_id")
        c_ib = put("dve", [c_id], lambda e: e.tensor_copy(identb[:, :], ident[:, :]), "c_dve")
        eng = ["dve", "pool"]
        c_q = [put(eng[i], [c_hf], lambda e, i=i: e.memset(QS[i][64:128, :, :].bitcast(F32), 0.0), f"c_s{i}") for i in range(2)]
        c_k = [put(eng[i], [c_q[i]], lambda e, i=i: e.memset(KS[i][64:96, :, :].bitcast(F32), 0.0), f"c_s{i}") for i in range(2)]
        c_o = [put(eng[i], [c_k[i]], lambda e, i=i: e.memset(KS[i][96:128, :, :].bitcast(F32), ONES), f"c_s{i}") for i in range(2)]
        c_v = [put("pool", [c_o[1]], lambda e, i=i: e.memset(VS[i][:, :, :, 8:16], 1.0), "c_v") for i in range(3)]
        c_p = put("dve", [], lambda e: e.memset(banks[4].ap[:, :], 0.0), "c_dve")
        banks[4].free = [c_p]

        prev = []
        for l in range(2):
            b0, b1 = banks[0], banks[1]
            if l:
                l_c = dma("sp", [prev[0]], cs[:, 2, :], cT[1], "l_c1")
                l_wm = [dma("act", [prev[1]], wms[n][:, 0:384], wm[1, :, 384 * n:384 * n + 384], f"l_wm1{n}")
                        for n in range(2)]
            th = put("act", [l_c], lambda e: e.activation(cs[:, 0, :], cs[:, 2, :], ACT.Tanh, scale=0.5), "m_th")
            s1 = put("dve", [th], lambda e: e.scalar_tensor_tensor(
                out=cs[:, 1, :], in0=cs[:, 0, :], scalar=1.0, in1=cs[:, 2, :], op0=ALU.add, op1=ALU.mult), "m_dve")
            s2 = put("dve", [s1], lambda e: e.tensor_scalar(cs[:, 0, :], cs[:, 1, :], 0.5, None, ALU.mult), "m_dve")
            for k in range(6):
                mm = put("pe", [s2] + l_wm + b0.free, lambda e, k=k: e.matmul(
                    b0.ap[:, 8 * k:8 * k + 8], wms[k // 3][:, 128 * (k % 3):128 * (k % 3) + 128], cs[:, 0, :],
                    start=True, stop=True), "m_pe")
            for n, k in enumerate((2, 5)):
                mg = put("pe", [s2] + b1.free, lambda e, n=n, k=k: e.matmul(
                    b1.ap[0:8, 128 * n:128 * n + 128], cs[:, 0, :], wms[k // 3][:, 128 * (k % 3):128 * (k % 3) + 128],
                    start=True, stop=True), "m_pe")
            cp = put("dve", [mm], lambda e, l=l: e.tensor_copy(mods[:, l, :, :], b0.ap[:, 0:48].rearrange(
                "p (k b) -> p k b", k=6)), "m_dve")
            for k in (1, 4):
                mod_ready = put("dve", [cp], lambda e, l=l, k=k: e.tensor_scalar(
                    mods[:, l, k, :], mods[:, l, k, :], 1.0, None, ALU.add), "m_dve")
            b0.free = [cp]
            g = put("dve", [mg], lambda e: e.tensor_copy(gat[:, 0, :, :], b1.ap[0:8, 0:256].rearrange(
                "p (k f) -> p k f", k=2)), "m_dve")
            b1.free = [g]
            g1 = put("dve", [g], lambda e: e.tensor_scalar(gat[:, 1, :, :], gat[:, 0, :, :], -1.0, None, ALU.mult), "m_dve")
            g2 = put("dve", [g1], lambda e: e.tensor_tensor(gat[:, 1, :, :], gat[:, 1, :, :], gat[:, 0, :, :], ALU.max), "m_dve")
            g3 = put("dve", [g2], lambda e: e.tensor_scalar(gat[:, 1, :, :], gat[:, 1, :, :], 0.25, None, ALU.max), "m_dve")
            g4 = put("dve", [g3], lambda e: e.tensor_scalar(gat[:, 2, :, :], gat[:, 0, :, :], 0.0, 2.0, ALU.is_ge, ALU.mult), "m_dve")
            g5 = put("dve", [g4], lambda e: e.tensor_scalar(gat[:, 2, :, :], gat[:, 2, :, :], -1.0, None, ALU.add), "m_dve")
            if l:
                g5 = put("dve", [g5, last["gst", 0]], lambda e: e.tensor_tensor(
                    gat[:, 3, :, :], gat[:, 2, :, :], gat[:, 1, :, :], ALU.mult), "m_dve")
            else:
                g5 = put("dve", [g5], lambda e: e.tensor_tensor(
                    gat[:, 3, :, :], gat[:, 2, :, :], gat[:, 1, :, :], ALU.mult), "m_dve")
            last["gst", l] = dma("sp", [g5], d_g[l], gat[:, 3, :, :], f"m_gst{l}")
            last["mod", l] = mod_ready
            prev = [mg, mg]
        setup = q.stream

        def norm_turn(w, i, l, b, ks, kc, bank, x_ready, xn_free, hT_free):
            seg(2.0)
            for t in range(NT):
                a = put("dve", [x_ready] if t == 0 else [], lambda e, t=t: e.bn_stats(
                    st6[:, i, t, :], X[:, NT * b + t, :]), w + "_ln")
            for t in range(NT):
                a2 = put("dve", [a], lambda e, t=t: e.bn_aggr(mv[:, i, t, :], st6[:, i, t, :]), w + "_ln")
            v = put("pool", [a2], lambda e: e.tensor_scalar(rs[:, i, 0, :], mv[:, i, :, 1], EPS, None, ALU.add), w + "_rs")
            r = put("pool", [v, c_hf], lambda e: e.tensor_tensor(rs[:, i, 1, :], rs[:, i, 0, :], half[:, :], ALU.pow), w + "_rs")
            seg(0.5)
            for t in range(NT):
                n = put("dve", [r, xn_free], lambda e, t=t: e.tensor_scalar(
                    xn[i][:, t, :], X[:, NT * b + t, :], mv[:, i, t, 0:1], rs[:, i, 1, t:t + 1],
                    ALU.subtract, ALU.mult), w + "_ln")
            seg(1.0)
            for t in range(NT):
                tr = put("pe", [n, c_id] + bank.free, lambda e, t=t: e.transpose(
                    bank.ap[:, 128 * t:128 * t + 128], xn[i][:, t, :], ident[:, :]), w + "_tr")
            hh = put("act", [tr, hT_free, last["mod", l]], lambda e: e.activation(
                hT[i][:, :], bank.ap[:, :], ACT.Identity, bias=mods[:, l, ks, b:b + 1],
                scale=mods[:, l, kc, b:b + 1]), w + "_hT")
            bank.free = [hh]
            return tr, hh

        fr = {"xn0": None, "xn1": None, "hT0": None, "hT1": None, "lat": None, "sp": [None, None],
              "sr": None, "V": [None] * 3, "G": [None] * 4, "stackA": {}, "stackB": {}}

        def stage_p(i):
            l, b, bank = i // NB, i % NB, banks[0]
            q.open()
            seg(0.1)
            gt = GT[i % 4]
            last["G", i] = dma("sp", [fr["G"][i % 4], last["gst", l]], gt[:, :, :],
                               d_g[l, b].partition_broadcast(128), f"p_g{i % 4}")
            x_ready = last["x", b] if l == 0 else last["xf", i - NB]
            tr, hh = norm_turn("p", 0, l, b, 0, 1, bank, x_ready, fr["xn0"], fr["hT0"])
            W, ws, lw = (W0, w0s, l_w0) if l == 0 else (W1, w1s, l_w1)
            src, sready = hT[0], hh
            if l == 1:
                seg(1.0)
                m = put("pe", [hh, lw] + bank.free, lambda e: e.matmul(
                    bank.ap[:, :], ws[:, W["lat"]:W["lat"] + 128], hT[0][:, :], start=True, stop=True), "p_lat")
                sready = put("act", [m], lambda e: e.activation(lat[:, :], bank.ap[:, :], ACT.Copy), "p_latc")
                bank.free = [sready]
                fr["hT0"] = m
                src = lat
            for n, (name, dd) in enumerate((("q", d_q), ("k", d_k))):
                seg(1.0)
                m = put("pe", [sready, lw] + bank.free, lambda e, name=name, src=src: e.matmul(
                    bank.ap[:, :], ws[:, W[name]:W[name] + 128], src[:, :], start=True, stop=True), "p_qk")
                s = sp[n]
                hi = put("act", [m, fr["sp"][n]], lambda e, s=s: e.activation(s[:, 0, :], bank.ap[:, :], ACT.Copy), "p_hi")
                rr = put("dve", [hi, m, fr["sr"]], lambda e, s=s, n=n: e.tensor_tensor(
                    sr[:, :], bank.ap[:, :], s[:, 0, :], ALU.subtract), "p_res")
                bank.free = [hi, rr]
                mi = put("pool", [rr, fr["sp"][n]], lambda e, s=s, n=n: e.tensor_scalar(
                    s[:, 1, :], sr[:, :], 1.0, None, ALU.mult), "p_part")
                lo = put("pool", [mi], lambda e, s=s, n=n: e.tensor_tensor(
                    s[:, 2, :], sr[:, :], s[:, 1, :], ALU.subtract), "p_part")
                fr["sr"] = lo
                for k in range(3):
                    st = dma("sp", [hi, lo, last.get(("stk", i - 2, 3))],
                             dd[i % 2][k].rearrange("d (h t) -> h d t", h=H), s[:, k, :], f"p_st{name}{i % 2}")
                fr["sp"][n] = st
                last["parts" + name, i] = st
            seg(1.0)
            for t in range(NT):
                m = put("pe", [sready, lw] + bank.free, lambda e, t=t, src=src: e.matmul(
                    bank.ap[:, 128 * t:128 * t + 128], src[:, 128 * t:128 * t + 128],
                    ws[:, W["v"]:W["v"] + 128], start=True, stop=True), "p_v")
            vv = put("act", [m, fr["V"][i % 3], c_v[i % 3]], lambda e: e.activation(
                VS[i % 3][:, :, :, 0:8], bank.ap[:, :].rearrange("p (t h d) -> p t h d", t=NT, h=H), ACT.Copy), "p_vc")
            bank.free = [vv]
            last["V", i] = vv
            if l == 0:
                fr["hT0"] = m
            fr["xn0"] = m
            return q.stream

        def load_stacks(i, g):
            free = last.get(("sT", i - 2, g))
            w = [free, last["partsq", i], last["partsk", i], c_q[i % 2], c_k[i % 2]]
            sem, hs, n = f"l_st{i % 2}{g}", slice(4 * g, 4 * g + 4), 4 * S
            kv, qv = d_k[i % 2], d_q[i % 2]
            dma("sp", w, KS[i % 2][0:72, hs, :], bass.AP(
                tensor=kv.tensor, offset=kv.offset + g * n, ap=[[0, 3], [H * S, 3 * DH], [1, n]]), sem)
            for a in range(3):
                mk = dma("sp", w, QS[i % 2][24 * a:24 * a + 24, hs, :], bass.AP(
                    tensor=qv.tensor, offset=qv.offset + a * DH * H * S + g * n,
                    ap=[[0, 3], [H * S, DH], [1, n]]), sem)
            last["stk", i, g] = mk

        def stage_a(i, end):
            l = i // NB
            early, late = Ring([banks[1], banks[5]]), Ring([banks[1], banks[0]])
            if i >= NB + 2:
                early, late = Ring([banks[1], banks[6]]), Ring([banks[1], banks[6], banks[0]])
            pool = early
            Q, K = QS[i % 2], KS[i % 2]
            q.open()
            for h in range(H):
                for t in range(NT):
                    n = 512 if l == 0 else 128 * (t + 1)
                    seg(n / 512)
                    if sum(w for w, _ in q.stream[:-1]) >= 0.245 / end * (64.5 if l == 0 else 40.5):
                        pool = late
                    bank = pool.next()
                    m = put("pe", [last["stk", i, h // 4], c_o[i % 2], c_q[i % 2], c_k[i % 2]] + bank.free,
                            lambda e, h=h, t=t, n=n, bank=bank: e.matmul(
                                bank.ap[:, 0:n], Q[0:KA, h, 128 * t:128 * t + 128], K[0:KA, h, 0:n],
                                start=True, stop=(l == 0)), "a_mm")
                    if l:
                        m = put("pe", [c_ib, c_mq], lambda e, n=n, bank=bank: e.matmul(
                            bank.ap[:, n - 128:n], identb[:, :], maskq[:, :], start=False, stop=True), "a_mm")
                    r = put("dve", [m, fr.get("nm")], lambda e, h=h, t=t, n=n, bank=bank: e.tensor_reduce(
                        nm[:, 4 * h + t:4 * h + t + 1], bank.ap[:, 0:n], AX.X, ALU.max, negate=True), "a_max")
                    bank.free = [r]
            seg(0.5)
            bank = pool.next()
            tr = put("pe", [r, c_id] + bank.free, lambda e: e.transpose(
                bank.ap[0:64, 0:128], nm[:, :], ident[:, :]), "a_tr")
            fr["nm"] = tr
            hi = put("act", [tr, fr.get("nmp")], lambda e: e.activation(nmp[:, 0, :], bank.ap[0:64, 0:128], ACT.Copy), "a_hi")
            rr = put("dve", [hi, fr.get("nmr")], lambda e: e.tensor_tensor(
                nmr[:, :], bank.ap[0:64, 0:128], nmp[:, 0, :], ALU.subtract), "a_res")
            bank.free = [hi, rr]
            mi = put("dve", [rr], lambda e: e.tensor_copy(nmp[:, 1, :], nmr[:, :]), "a_res")
            lo = put("dve", [mi], lambda e: e.tensor_tensor(nmp[:, 2, :], nmr[:, :], nmp[:, 1, :], ALU.subtract), "a_res")
            fr["nmr"] = lo
            st = dma("sp", [lo, hi], d_m[i % 2].rearrange("k r c -> r k c"), nmp[:, :, :], f"a_st{i % 2}")
            fr["nmp"] = st
            last["M", i] = dma("sp", [st, last.get(("sT", i - 2, 3))], QS[i % 2][96:99, :, :],
                               d_m[i % 2].rearrange("k (h t) c -> k h (t c)", h=H), f"a_ld{i % 2}")
            return q.stream

        ering = Ring(list(range(NE_)))
        efree = [None] * NE_

        def stage_b(i):
            l, pool, pv = i // NB, Ring([banks[2], banks[3]]), banks[4]
            Q, K, V = QS[i % 2], KS[i % 2], VS[i % 3]
            scale = SC1 if l else SC0
            q.open()
            lag, ust = [], []

            def attend(g, j, q0, slots):
                for a, (s, ex) in enumerate(slots):
                    m = put("pe", [ex, last["V", i], c_p] + (pv.free if j == 0 else []),
                            lambda e, a=a, s=s, j=j, h=4 * g + a: e.matmul(
                                pv.ap[32 * a:32 * a + 16, q0:512], V[:, j, h, :], ES[s][:, 0:512 - q0],
                                start=(j == 0), stop=(j == NT - 1), skip_group_check=True), "b_pv")
                    efree[s] = m
                if j == NT - 1:
                    u = put("act", [m, fr.get(("U", g % 2))], lambda e: e.activation(US[g % 2][:, :], pv.ap[:, :], ACT.Copy), "b_u")
                    pv.free = [u]
                    for a in range(4):
                        last["U", i] = fr["U", g % 2] = dma("sp", [u], d_u[i % 2][g, a], US[g % 2][32 * a:32 * a + 16, :],
                                                            f"b_stu{i % 2}{g}")
                    ust.append(last["U", i])
                    if i + 2 < 2 * NB:
                        load_stacks(i + 2, g)
                if (g, j) == (3, NT - 1):
                    fr["V"][i % 3] = m

            for g in range(4):
                for j in range(NT):
                    q0 = 0 if l == 0 else 128 * j
                    slots = []
                    for a in range(4):
                        h = 4 * g + a
                        seg((512 - q0) / 512)
                        bank = pool.next()
                        m = put("pe", [last["M", i]] + bank.free, lambda e, h=h, j=j, bank=bank, q0=q0: e.matmul(
                            bank.ap[:, 0:512 - q0], K[0:KB, h, 128 * j:128 * j + 128], Q[0:KB, h, q0:512],
                            start=True, stop=(l == 0)), "b_mm")
                        last["sT", i, g] = m
                        if l:
                            m = put("pe", [], lambda e, bank=bank: e.matmul(
                                bank.ap[:, 0:128], identb[:, :], maskk[:, :], start=False, stop=True), "b_mm")
                        s = ering.next()
                        ex = put("act", [m, efree[s]], lambda e, s=s, bank=bank, q0=q0: e.activation(
                            ES[s][:, 0:512 - q0], bank.ap[:, 0:512 - q0], ACT.Exp, scale=scale), "b_exp")
                        bank.free = [ex]
                        slots.append((s, ex))
                    if lag:
                        seg(1.0)
                        attend(*lag.pop())
                    lag.append((g, j, q0, slots))
            seg(1.0)
            attend(*lag.pop())
            seg(0.1)
            uv = d_u[i % 2].rearrange("g a r t -> (g a) r t")
            ld = dma("sp", ust + [fr.get("DC")], DC[:, 0, :], uv[:, 8, :].rearrange("h (b c) -> h b c", b=8), "b_ldd")
            last["OT", i] = dma("sp", ust + [fr.get("OT")], OT[:, :], uv[:, 0:8, :], "b_ldo")
            last["DC", i] = ld
            return q.stream

        def stage_t(i):
            l, b, bank = i // NB, i % NB, banks[7]
            W, ws, lw = (W0, w0s, l_w0) if l == 0 else (W1, w1s, l_w1)
            q.open()
            seg(1.0)
            rc = put("dve", [last["DC", i], fr.get("DC2")], lambda e: e.reciprocal(DC[:, 1, :], DC[:, 0, :]), "b_rc")
            fr["DC"] = rc
            s2 = dma("sp", [rc], d_r[i % 2].rearrange("h (b c) -> (h b) c", b=8), DC[:, 1, :], "b_str")
            fr["DC2"] = s2
            rv = d_r[i % 2]
            last["DR", i] = dma("sp", [s2, fr.get("DR")], DR[:, :], bass.AP(
                tensor=rv.tensor, offset=rv.offset, ap=[[S, H], [0, DH], [1, S]]), "b_ldr")
            seg(0.5)
            o = put("pool", [last["OT", i], last["DR", i]], lambda e: e.tensor_tensor(
                OT[:, :], OT[:, :], DR[:, :], ALU.mult), "t_o")
            fr["DR"] = o
            seg(1.0)
            for t in range(NT):
                m = put("pe", [o, lw] + bank.free, lambda e, t=t: e.matmul(
                    bank.ap[:, 128 * t:128 * t + 128], OT[:, 128 * t:128 * t + 128],
                    ws[:, W["o"]:W["o"] + 128], start=True, stop=True), "t_mm")
            fr["OT"] = m
            bb = bos[:, l:l + 1, :].broadcast_to([128, NT, 128])
            a = put("dve", [m, l_bo, ytf[0]], lambda e: e.tensor_tensor(
                pt[:, :, :], bank.ap[:, :].rearrange("p (t f) -> p t f", t=NT), bb, ALU.add), "t_b")
            bank.free = [a]
            gg = GT[i % 4][:, 0:1, :].broadcast_to([128, NT, 128])
            g = put("pool", [a, last["G", i]], lambda e: e.tensor_tensor(pt[:, :, :], pt[:, :, :], gg, ALU.mult), "t_x")
            xs = X[:, NT * b:NT * b + NT, :]
            last["xt", i] = put("pool", [g], lambda e: e.tensor_tensor(xs, xs, pt[:, :, :], ALU.add), "t_x")
            return q.stream

        ub = Ring([0, 1])
        hb = Ring(list(range(NHD)))
        ufree, hfree, ytf = [None] * 2, [prev[0]] * NHD, [None] * 2
        yring = Ring([0, 1])

        def stage_f(i):
            l, b = i // NB, i % NB
            W, ws, lw = (W0, w0s, l_w0) if l == 0 else (W1, w1s, l_w1)
            pool, yb = Ring([banks[5], banks[6]] if l == 0 else [banks[5]]), banks[7]
            q.open()
            tr, hh = norm_turn("f", 1, l, b, 3, 4, pool.next(), last["xt", i], fr.get("ya"), fr["hT1"])
            seg(2.0)
            bank = pool.next()
            for t in range(NT):
                m = put("pe", [hh, lw] + bank.free, lambda e, t=t: e.matmul(
                    bank.ap[:, E * t:E * t + E], hT[1][:, 128 * t:128 * t + 128], ws[:, W["g"]:W["g"] + E],
                    start=True, stop=True), "f_g")
            c0 = put("dve", [m], lambda e: e.tensor_copy(lg[:, 0, :, :], bank.ap[:, 0:NT * E].rearrange(
                "p (t e) -> p t e", t=NT)), "f_r")
            bank.free = [c0]
            seg(0.5)
            c1 = put("dve", [c0], lambda e: e.tensor_reduce(sm[:, 0, :], lg[:, 0, :, :], AX.X, ALU.max), "f_r")
            c2 = put("dve", [c1], lambda e: e.tensor_tensor(
                lg[:, 1, :, :], lg[:, 0, :, :], sm[:, 0, :].unsqueeze(2).broadcast_to([128, NT, E]), ALU.subtract), "f_r")
            ex = put("act", [c2], lambda e: e.activation(lg[:, 2, :, :], lg[:, 1, :, :], ACT.Exp), "f_e")
            seg(0.5)
            c3 = put("dve", [ex], lambda e: e.tensor_reduce(sm[:, 1, :], lg[:, 2, :, :], AX.X, ALU.add), "f_r")
            c4 = put("dve", [c3], lambda e: e.reciprocal(sm[:, 2, :], sm[:, 1, :]), "f_r")
            c5 = put("dve", [c4], lambda e: e.tensor_tensor(
                lg[:, 3, :, :], lg[:, 2, :, :], sm[:, 2, :].unsqueeze(2).broadcast_to([128, NT, E]), ALU.mult), "f_r")
            for t in range(NT):
                c6 = put("dve", [c5], lambda e, t=t: e.max(m8[:, t, :], lg[:, 3, t, :]), "f_r")
            seg(0.5)
            for t in range(NT):
                c7 = put("dve", [c6], lambda e, t=t: e.max_index(i8[:, t, :], m8[:, t, :], lg[:, 3, t, :]), "f_r")
            c8 = put("dve", [c7], lambda e: e.tensor_copy(if8[:, :, :], i8[:, :, :]), "f_r")
            seg(0.5)
            io = iota8[:, :].unsqueeze(1).broadcast_to([128, NT, E])
            for k in range(2):
                c9 = put("dve", [c8, c_io], lambda e, k=k: e.tensor_tensor(
                    lg[:, 4 + k, :, :], io, if8[:, :, k:k + 1].broadcast_to([128, NT, E]), ALU.is_equal), "f_r")
            for k in range(2):
                c10 = put("dve", [c9], lambda e, k=k: e.tensor_tensor(
                    lg[:, 4 + k, :, :], lg[:, 4 + k, :, :], m8[:, :, k:k + 1].broadcast_to([128, NT, E]), ALU.mult), "f_r")
            comb = put("dve", [c10, fr.get("comb")], lambda e: e.tensor_tensor(
                lg[:, 0, :, :], lg[:, 4, :, :], lg[:, 5, :, :], ALU.add), "f_r")
            if l == 0:
                comb = put("dve", [comb], lambda e: e.tensor_scalar(lg[:, 0, :, :], lg[:, 0, :, :], 0.5, None, ALU.mult), "f_r")

            yacc = [None]

            def down(e_, hids, w2, off):
                seg(0.0)
                for t in range(NT):
                    for n, (s, ready) in enumerate(hids):
                        m = put("pe", [ready, l_f2 if l == 0 else last["r2"]] + (yb.free if t == 0 and n == 0 else []),
                                lambda e, t=t, n=n, s=s, rn=(96 if n == 2 else 128): e.matmul(
                                    yb.ap[:, 128 * t:128 * t + 128], hd[s][0:rn, 128 * t:128 * t + 128],
                                    w2[0:rn, off + n, :], start=(n == 0), stop=(n == len(hids) - 1)), "f_dn")
                        hfree[s] = m
                    seg(0.25 * len(hids))
                yv = yb.ap[:, :].rearrange("p (t f) -> p t f", t=NT)
                if e_ == E:
                    d = put("dve", [m, fr.get("ya")], lambda e: e.tensor_scalar(ya[:, :, :], yv, 0.5, None, ALU.mult), "f_y")
                    yb.free = [d]
                    yacc[0] = d
                    return
                k = yring.next()
                cb = lg[:, 0, :, e_].unsqueeze(2).broadcast_to([128, NT, 128])
                if l == 1 and e_ == 0:
                    d = put("dve", [m, comb, fr.get("ya")], lambda e: e.tensor_tensor(ya[:, :, :], yv, cb, ALU.mult), "f_y")
                    yacc[0] = d
                else:
                    d = put("dve", [m, comb, ytf[k]], lambda e: e.tensor_tensor(yt[k][:, :, :], yv, cb, ALU.mult), "f_y")
                    yacc[0] = ytf[k] = put("pool", [d, yacc[0]], lambda e, k=k: e.tensor_tensor(
                        ya[:, :, :], ya[:, :, :], yt[k][:, :, :], ALU.add), "f_ya")
                yb.free = [d]
                if e_ == E - 1:
                    fr["comb"] = d

            pending = None
            if l == 0:
                for e_ in [E] + list(range(E)):
                    off, nch = 3 * e_, (2 if e_ == E else 3)
                    hids = []
                    for c in range(nch):
                        ba, bb_ = pool.next(), pool.next()
                        seg(2.0)
                        r0, rn = 352 * e_ + 128 * c, (96 if c == 2 else 128)
                        ma = put("pe", [hh, l_f1] + ba.free, lambda e, ba=ba, r0=r0, rn=rn: e.matmul(
                            ba.ap[0:rn, :], f1[:, r0:r0 + rn], hT[1][:, :], start=True, stop=True), "f_up")
                        mb = put("pe", [l_f3] + bb_.free, lambda e, bb_=bb_, r0=r0, rn=rn: e.matmul(
                            bb_.ap[0:rn, :], f3[:, r0:r0 + rn], hT[1][:, :], start=True, stop=True), "f_up")
                        k, s = ub.next(), hb.next()
                        th = put("act", [ma, ufree[k]], lambda e, k=k, ba=ba, rn=rn: e.activation(
                            tt[k][0:rn, :], ba.ap[0:rn, :], ACT.Tanh, scale=0.5), "f_th")
                        u = put("dve", [th, ma, hfree[s]], lambda e, k=k, s=s, ba=ba, rn=rn: e.scalar_tensor_tensor(
                            out=hd[s][0:rn, :], in0=tt[k][0:rn, :], scalar=1.0, in1=ba.ap[0:rn, :],
                            op0=ALU.add, op1=ALU.mult), "f_u")
                        hm = put("dve", [u, mb], lambda e, s=s, bb_=bb_, rn=rn: e.tensor_tensor(
                            hd[s][0:rn, :], bb_.ap[0:rn, :], hd[s][0:rn, :], ALU.mult), "f_u")
                        ufree[k] = u
                        ba.free, bb_.free = [u], [hm]
                        hids.append((s, hm))
                        fr["hT1"] = mb
                        if c == 0 and pending:
                            down(*pending)
                            pending = None
                    pending = (e_, hids, f2, off)
                down(*pending)
                if i == NB - 1:
                    last["r1"] = dma("sp", [fr["hT1"]], r1, wr1, "l_r1")
                    last["r2"] = dma("sp", [fr["hT1"]], r2, wr2, "l_r2")
            else:
                for e_ in range(E):
                    ba = pool.next()
                    seg(1.0)
                    ma = put("pe", [hh, last["r1"]] + ba.free, lambda e, ba=ba, e_=e_: e.matmul(
                        ba.ap[:, :], r1[:, e_, :], hT[1][:, :], start=True, stop=True), "f_up")
                    fr["hT1"] = ma
                    k, s = ub.next(), hb.next()
                    re = put("act", [ma, ufree[k]], lambda e, k=k, ba=ba: e.activation(
                        tt[k][:, :], ba.ap[:, :], ACT.Relu), "f_th")
                    ba.free = [re]
                    hm = put("dve", [re, hfree[s]], lambda e, k=k, s=s: e.tensor_tensor(
                        hd[s][:, :], tt[k][:, :], tt[k][:, :], ALU.mult), "f_u")
                    ufree[k] = hm
                    if pending:
                        down(*pending)
                    pending = (e_, [(s, hm)], r2, e_)
                down(*pending)
            seg(0.0)
            gg = GT[i % 4][:, 1:2, :].broadcast_to([128, NT, 128])
            g = put("pool", [yacc[0]], lambda e: e.tensor_tensor(ya[:, :, :], ya[:, :, :], gg, ALU.mult), "f_x")
            xs = X[:, NT * b:NT * b + NT, :]
            fx = put("pool", [g], lambda e: e.tensor_tensor(xs, xs, ya[:, :, :], ALU.add), "f_x")
            fr["ya"] = fx
            fr["G"][i % 4] = fx
            last["xf", i] = fx
            if l == 1:
                ov = out.rearrange("b (t p) d -> p (b t) d", p=128)
                last["out", b] = dma("sp", [fx], ov[:, NT * b:NT * b + NT, :], xs, "f_out")
            return q.stream

        order = merge([(setup, 0, 1)])
        N = 2 * NB
        for s in range(N + 3):
            parts = []
            if s < N:
                parts.append((stage_p(s), 0.0, 0.24))
            if 0 <= s - 2 < N:
                parts.append((stage_b(s - 2), 0.04, 1.0))
            if 0 <= s - 1 < N:
                end = 0.9 if s - 1 < NB else 0.86
                parts.append((stage_a(s - 1, end), 0.0, end))
            if 0 <= s - 3 < N:
                parts.append((stage_t(s - 3), 0.14, 0.25 if s - 3 < NB else 0.3))
                parts.append((stage_f(s - 3), 0.26 if s - 3 < NB else 0.31, 1.0))
            order += merge(parts)
            if s < 2:
                q.open()
                seg(0)
                for g in range(4):
                    load_stacks(s, g)
                order += merge([(q.stream, 0, 1)])
        q.open()
        seg(0)
        order += [("sp", [last["out", NB - 1]], None, None, 0)]

        issued = {}
        for who, waits, fn, sem, by in order:
            assert all(issued.get(w.sem, 0) >= w.value for w in waits), (who, sem)
            issued[sem] = issued.get(sem, 0) + by
        sems = {name: ctx.enter_context(nc.semaphore(name)) for name in q.count}
        block = ctx.enter_context(nc.Block())

        def issue(name, eng):
            seen = {}
            for who, waits, fn, sem, by in order:
                if who != name:
                    continue
                for w in waits:
                    if seen.get(w.sem, 0) < w.value:
                        eng.wait_ge(sems[w.sem], w.value)
                        seen[w.sem] = w.value
                if fn is None:
                    continue
                ins = fn(eng)
                if sem is not None:
                    ins.then_inc(sems[sem], by)

        @block.tensor
        def _(eng):
            issue("pe", eng)

        @block.vector
        def _(eng):
            issue("dve", eng)

        @block.scalar
        def _(eng):
            issue("act", eng)

        @block.gpsimd
        def _(eng):
            issue("pool", eng)

        @block.sync
        def _(eng):
            issue("sp", eng)


def kernel(**inputs):
    import numpy as _np
    import concourse.bacc as _bacc
    from concourse import mybir as _mybir
    from concourse.bass_utils import run_bass_kernel_spmd as _run

    x = {k: _np.asarray(v) for k, v in inputs.items()}
    f = x["L0_attn_x"].dtype

    def cols(w, n):
        out = _np.zeros((128, n), w.dtype)
        out[:w.shape[0], :w.shape[1]] = w
        return out

    wqkv = x["L0_attn_w_qkv"]
    w0 = _np.concatenate([wqkv[0:128].T, wqkv[128:256].T, wqkv[256:384].T,
                          x["L0_attn_w_out"].T, x["L0_ffn_gate_w"].T], 1)
    lat = cols(_np.concatenate([x["L1_attn_wq_lat"], x["L1_attn_wk_lat"], x["L1_attn_wv_lat"]], 1), 128)
    heads = []
    for n, name in enumerate(("q", "k", "v")):
        h = _np.zeros((128, 128), f)
        h[32 * n:32 * n + 32] = x[f"L1_attn_w{name}_heads"]
        heads.append(h)
    w1 = _np.concatenate([lat] + heads + [x["L1_attn_w_proj"], x["L1_ffn_Wr"]], 1)

    def up(w, s):
        out = _np.zeros((128, 8 * 352 + 256), w.dtype)
        out[:, :8 * 352] = w.transpose(1, 0, 2).reshape(128, 8 * 352)
        out[:, 8 * 352:8 * 352 + 192] = s
        return out

    def down(w, s):
        out = _np.zeros((26, 128, 128), w.dtype)
        a = _np.zeros((8, 384, 128), w.dtype)
        a[:, :352] = w
        out[:24] = a.reshape(24, 128, 128)
        b = _np.zeros((256, 128), w.dtype)
        b[:192] = s
        out[24:] = b.reshape(2, 128, 128)
        return out.transpose(1, 0, 2)

    args = {
        "xin": x["L0_attn_x"],
        "cT": _np.stack([x["L0_c"].T, x["L1_c"].T]),
        "wm": _np.stack([x["L0_wmod"], x["L1_wmod"]]),
        "w0": w0,
        "wf1": up(x["L0_ffn_w1"], x["L0_ffn_sw1"]),
        "wf3": up(x["L0_ffn_w3"], x["L0_ffn_sw3"]),
        "wf2": down(x["L0_ffn_w2"], x["L0_ffn_sw2"]),
        "w1": w1,
        "wr1": x["L1_ffn_W1"].transpose(1, 0, 2),
        "wr2": x["L1_ffn_W2"].transpose(1, 0, 2),
        "bo": _np.stack([x["L0_attn_b_out"], x["L1_attn_b_proj"]]),
    }
    nc = _bacc.Bacc("TRN2", target_bir_lowering=False, num_devices=1)
    arrays, aps = {}, []
    for name, a in args.items():
        a = _np.ascontiguousarray(a)
        arrays[name] = a
        aps.append(nc.dram_tensor(name, a.shape, _mybir.dt.from_np(a.dtype), kind="ExternalInput").ap())
    o = nc.dram_tensor("y", (8, 512, 128), _mybir.dt.float32, kind="ExternalOutput").ap()
    program(nc, *aps, o)
    r = _run(nc, [arrays], core_ids=[0])
    return r.results[0]["y"]
```

```python
from contextlib import ExitStack

import numpy as np
import concourse.bass as bass
from concourse import mybir

F32 = mybir.dt.float32
BF16 = mybir.dt.bfloat16
U32 = mybir.dt.uint32
ALU = mybir.AluOpType
ACT = mybir.ActivationFunctionType
AX = mybir.AxisListType

NB, S, D = 8, 512, 128
NT = S // 128
H, DH = 16, 8
E = 8
NPROD = 9
NSLOT = 6
NMT = 2 * (2 * S) // 128 + E - 1
KA, KB = 96, 128
BIG = -float(2.0 ** 126)
SC0 = float(128 ** (-0.5))
SC1 = float(1.0 / np.sqrt(8).astype(np.float32))
EPS = 1e-5
ONES = float(np.array([0x3F803F80], np.uint32).view(np.float32)[0])

W0 = {"q": 0, "k": 128, "v": 256, "o": 384, "g": 512}
W0N = 520
W1 = {"lat": 0, "q": 128, "k": 256, "v": 384, "o": 512, "g": 640}
W1N = 648


class Mark:

    def __init__(self, sem, value):
        self.sem, self.value = sem, value


class Queues:

    def __init__(self):
        self.count = {}
        self.stream = None

    def open(self):
        self.stream = []

    def seg(self, weight):
        self.stream.append((weight, []))

    def put(self, engine, waits, fn, sem=None, by=1):
        self.stream[-1][1].append((engine, [w for w in waits if w is not None], fn, sem, by))
        if sem is None:
            return None
        self.count[sem] = self.count.get(sem, 0) + by
        return Mark(sem, self.count[sem])

    def dma(self, engine, waits, out, in_, sem):
        return self.put(engine, waits, lambda e: e.dma_start(out, in_), sem, 16)


class Bank:

    def __init__(self, ap):
        self.ap, self.free = ap, []


class Places:

    def __init__(self, n, mark):
        self.idle = [(k, mark) for k in range(n)]

    def take(self):
        return self.idle.pop(0)

    def give(self, k, mark):
        self.idle.append((k, mark))


class Ring:
    def __init__(self, items):
        self.items, self.n = items, 0

    def next(self):
        self.n += 1
        return self.items[(self.n - 1) % len(self.items)]


def merge(parts):
    keyed = []
    for k, (stream, a, b) in enumerate(parts):
        total = sum(w for w, _ in stream) or 1.0
        at = 0.0
        for n, (w, ins) in enumerate(stream):
            keyed.append((a + (b - a) * at / total, k, n, ins))
            at += w
    keyed.sort(key=lambda x: x[:3])
    return [i for x in keyed for i in x[3]]


def program(nc, xin, cT, wm, w0, wf1, wf3, wf2, w1, wr1, wr2, bo, out):
    ctx = ExitStack()
    with ctx:
        def sb(name, shape, dt=F32):
            return ctx.enter_context(nc.sbuf_tensor(name, shape, dt))

        def ps(name, shape, dt=F32):
            return ctx.enter_context(nc.psum_tensor(name, shape, dt))

        def dram(name, shape, dt=F32):
            return nc.dram_tensor(name, shape, dt, kind="Internal").ap()

        X = sb("X", [128, NB * NT, D])
        w0s = sb("w0s", [128, W0N])
        w1s = sb("w1s", [128, W1N])
        f1 = sb("f1", [128, 8 * 352 + 256])
        f3 = sb("f3", [128, 8 * 352 + 256])
        f2 = sb("f2", [128, E * 3 + 2, 128])
        r1 = sb("r1", [128, E, 128])
        r2 = sb("r2", [128, E, 128])
        cs = sb("cs", [128, 3, NB])
        mods = sb("mods", [128, 2, 6, NB])
        bos = sb("bos", [128, 2, 128])
        ident = sb("ident", [128, 128])
        identb = sb("identb", [128, 128], BF16)
        maskq = sb("maskq", [128, 128], BF16)
        maskk = sb("maskk", [128, 128], BF16)
        iota8 = sb("iota8", [128, E])
        half = sb("half", [128, NT])
        QS = sb("QS", [128, NSLOT, 4 * S], BF16)
        KS = sb("KS", [128, NSLOT, 4 * S], BF16)

        def stack(M, i, h):
            return M[:, (4 * i + h // 4) % NSLOT, S * (h % 4):S * (h % 4) + S]

        VS = [sb(f"VS{i}", [128, NT, H, 16]) for i in range(3)]
        NE_ = 8
        ES = [sb(f"ES{i}", [128, S]) for i in range(NE_)]
        US = [sb(f"US{i}", [128, S]) for i in range(2)]
        OT = sb("OT", [128, S])
        DR = sb("DR", [128, S])
        DC = sb("DC", [128, 2, 64])
        nm = sb("nm", [128, 64])
        st6 = sb("st6", [128, 2, NT, 6])
        mv = sb("mv", [128, 2, NT, 2])
        rs = sb("rs", [128, 2, 2, NT])
        ya = sb("ya", [128, NT, 128])
        lat = sb("lat", [128, S])
        xn = [lat[:, :].rearrange("p (t f) -> p t f", t=NT), ya[:, :, :]]
        hT = [sb(f"hT{i}", [128, S]) for i in range(2)]
        sp = [sb(f"sp{i}", [128, 3, S], BF16) for i in range(2)]
        sr = sb("sr", [128, S])
        nmp, nmr = sp[1][0:64, :, 0:128], sr[0:64, 0:128]
        GT = [sb(f"GT{i}", [128, 4, 128]) for i in range(2)]
        GC = sb("GC", [128, 128])
        hx = [sb(f"hx{i}", [128, NT, D]) for i in range(2)]
        hs = sb("hs", [128, 4, D])
        ys = sb("ys", [128, 4, D])
        gat = [hx[0][0:NB, :, :], hx[1][0:NB, :, :], ys[0:NB, :, :]]
        hsT = [sb(f"hsT{i}", [128, 512]) for i in range(2)]
        cv = sb("cv", [128, NT, D])
        gr = [sb(f"gr{i}", [128, D]) for i in range(4)]
        ohs = sb("ohs", [128, 2, 8, E])
        ohb = sb("ohb", [128, 64], BF16)
        wts = [sb(f"wts{i}", [128, 8, 2]) for i in range(2)]
        pos = [sb(f"pos{i}", [128, 2, 8], U32) for i in range(2)]
        tex = [sb(f"tex{i}", [128, 2, 24], U32) for i in range(2)]
        rt = sb("rt", [128, 6, 64])
        re_ = sb("re_", [128, 4, E])
        rj = sb("rj", [128, 24, E])
        te = sb("te", [128, 24])
        i24 = sb("i24", [128, 24])
        k128 = sb("k128", [128, E])
        seg8 = sb("seg8", [128, E, 8])
        one8 = sb("one8", [128, E])
        before = sb("before", [128, 128], BF16)
        onesb = sb("onesb", [128, 128], BF16)
        lg = sb("lg", [128, 6, NT, E])
        m8 = sb("m8", [128, NT, 8])
        i8 = sb("i8", [128, NT, 8], U32)
        if8 = sb("if8", [128, NT, 8])
        sm = sb("sm", [128, 3, NT])
        tt = [sb("tt", [128, S])]
        NHD = 4
        hd = [sb(f"hd{i}", [128, S]) for i in range(NHD)]
        wms = [hd[0], hd[1]]
        yt = [sb("yt", [128, NT, 128])]
        pt = yt[0]

        banks = [Bank(ps(f"ps{i}", [128, 512])) for i in range(8)]

        d_q = [dram(f"d_q{i}", [3, DH, H * S], BF16) for i in range(2)]
        d_k = [dram(f"d_k{i}", [3, DH, H * S], BF16) for i in range(2)]
        d_m = [dram(f"d_m{i}", [3, 64, 128], BF16) for i in range(2)]
        d_u = [dram(f"d_u{i}", [4, 4, 16, S]) for i in range(2)]
        d_r = [dram(f"d_r{i}", [H, S]) for i in range(2)]
        d_g = dram("d_g", [2, NB, 4, 128])
        d_h = [dram(f"d_h{i}", [NMT * 128, D]) for i in range(2)]
        d_y = [dram(f"d_y{i}", [NMT * 128, D]) for i in range(2)]

        q = Queues()
        put, dma, seg = q.put, q.dma, q.seg

        last = {}

        q.open()
        seg(0)
        xv = xin.rearrange("b (t p) d -> p (b t) d", p=128)
        for b in range(2):
            last["x", b] = dma("sp", [], X[:, NT * b:NT * b + NT, :], xv[:, NT * b:NT * b + NT, :], f"l_x{b}")
            if b == 0:
                l_c = dma("sp", [], cs[:, 2, :], cT[0], "l_c0")
                l_w0 = dma("sp", [], w0s[:, :], w0, "l_w0")
                l_wm = [dma("act", [], wms[n][:, 0:384], wm[0, :, 384 * n:384 * n + 384], f"l_wm0{n}") for n in range(2)]

        z = put("pool", [], lambda e: e.memset(ident[:, :], 0.0), "c_id")
        z1 = put("pool", [], lambda e: e.memset(maskq[:, :], 0.0), "c_id")
        z2 = put("pool", [], lambda e: e.memset(maskk[:, :], 0.0), "c_id")
        c_id = put("pool", [z], lambda e: e.affine_select(
            out=ident[:, :], in_=ident[:, :], compare_op=ALU.not_equal, fill=1.0, base=0,
            pattern=[[-1, 128]], channel_multiplier=1), "c_id")
        c_mq = put("pool", [z1], lambda e: e.affine_select(
            out=maskq[:, :], in_=maskq[:, :], compare_op=ALU.is_ge, fill=BIG, base=0,
            pattern=[[-1, 128]], channel_multiplier=1), "c_id")
        c_mk = put("pool", [z2], lambda e: e.affine_select(
            out=maskk[:, :], in_=maskk[:, :], compare_op=ALU.is_ge, fill=BIG, base=0,
            pattern=[[1, 128]], channel_multiplier=-1), "c_id")
        c_io = put("pool", [], lambda e: e.iota(iota8[:, :], [[1, E]], base=0, channel_multiplier=0,
                                                allow_small_or_imprecise_dtypes=True), "c_id")
        c_hf = put("pool", [], lambda e: e.memset(half[:, :], -0.5), "c_id")
        iota = lambda t, pat: put("pool", [], lambda e: e.iota(
            t, pat, base=0, channel_multiplier=0, allow_small_or_imprecise_dtypes=True), "c_id")
        iota(i24[:, :], [[1, 24]])
        iota(k128[:, :], [[128, E]])
        put("pool", [], lambda e: e.memset(one8[:, :], 1.0), "c_id")
        put("pool", [], lambda e: e.memset(onesb[:, :], 1.0), "c_id")
        z3 = put("pool", [], lambda e: e.memset(seg8[:, :, :], 1.0), "c_id")
        z4 = put("pool", [], lambda e: e.memset(before[:, :], 1.0), "c_id")
        put("pool", [z3], lambda e: e.memset(seg8[:, :, 0], 0.0), "c_id")
        c_rt = put("pool", [z4], lambda e: e.affine_select(
            out=before[:, :], in_=before[:, :], compare_op=ALU.is_gt, fill=0.0, base=0,
            pattern=[[1, 128]], channel_multiplier=-1), "c_id")
        z5 = put("pool", [], lambda e: e.memset(hs[:, :, :], 0.0), "c_id")
        c_ib = put("dve", [c_id], lambda e: e.tensor_copy(identb[:, :], ident[:, :]), "c_dve")
        c_q = put("pool", [z5], lambda e: e.memset(QS[64:128, :, :].bitcast(F32), 0.0), "c_st")
        c_k = put("dve", [], lambda e: e.memset(KS[64:96, :, :].bitcast(F32), 0.0), "c_dve")
        c_o = put("dve", [], lambda e: e.memset(KS[96:128, :, :].bitcast(F32), ONES), "c_dve")
        c_v = [put("pool", [c_q], lambda e, i=i: e.memset(VS[i][:, :, :, 8:16], 1.0), "c_v") for i in range(3)]
        c_p = put("dve", [], lambda e: e.memset(banks[4].ap[:, :], 0.0), "c_dve")
        banks[4].free = [c_p]

        setup = q.stream

        prev = []

        def modulation(l, l_c, l_wm):
            q.open()
            seg(1.0)
            b0, b1 = banks[5 * l], banks[1 + 5 * l]
            if l:
                l_c = dma("sp", [prev[0]], cs[:, 2, :], cT[1], "l_c1")
                l_wm = [dma("act", [prev[1]], wms[n][:, 0:384], wm[1, :, 384 * n:384 * n + 384], f"l_wm1{n}")
                        for n in range(2)]
                seg(1.0)
            th = put("act", [l_c], lambda e: e.activation(cs[:, 0, :], cs[:, 2, :], ACT.Tanh, scale=0.5), "m_th")
            s1 = put("dve", [th], lambda e: e.scalar_tensor_tensor(
                out=cs[:, 1, :], in0=cs[:, 0, :], scalar=1.0, in1=cs[:, 2, :], op0=ALU.add, op1=ALU.mult), "m_dve")
            s2 = put("dve", [s1], lambda e: e.tensor_scalar(cs[:, 0, :], cs[:, 1, :], 0.5, None, ALU.mult), "m_dve")
            for k in range(6):
                mm = put("pe", [s2] + l_wm + b0.free, lambda e, k=k: e.matmul(
                    b0.ap[:, 8 * k:8 * k + 8], wms[k // 3][:, 128 * (k % 3):128 * (k % 3) + 128], cs[:, 0, :],
                    start=True, stop=True), "m_pe")
            for n, k in enumerate((2, 3, 4, 5)):
                mg = put("pe", [s2] + b1.free, lambda e, n=n, k=k: e.matmul(
                    b1.ap[0:8, 128 * n:128 * n + 128], cs[:, 0, :], wms[k // 3][:, 128 * (k % 3):128 * (k % 3) + 128],
                    start=True, stop=True), "m_pe")
            cp = put("dve", [mm], lambda e, l=l: e.tensor_copy(mods[:, l, :, :], b0.ap[:, 0:48].rearrange(
                "p (k b) -> p k b", k=6)), "m_dve")
            for k in (1, 4):
                mod_ready = put("dve", [cp], lambda e, l=l, k=k: e.tensor_scalar(
                    mods[:, l, k, :], mods[:, l, k, :], 1.0, None, ALU.add), "m_dve")
            b0.free = [cp]
            g = put("dve", [mg, last.get(("gst", 0))], lambda e: e.tensor_copy(gat[0], b1.ap[0:8, :].rearrange(
                "p (k f) -> p k f", k=4)), "m_dve")
            b1.free = [g]
            g1 = put("dve", [g], lambda e: e.tensor_scalar(gat[1], gat[0], -1.0, None, ALU.mult), "m_dve")
            g2 = put("dve", [g1], lambda e: e.tensor_tensor(gat[1], gat[1], gat[0], ALU.max), "m_dve")
            g3 = put("dve", [g2], lambda e: e.tensor_scalar(gat[1], gat[1], 0.25, None, ALU.max), "m_dve")
            g4 = put("dve", [g3], lambda e: e.tensor_scalar(gat[2], gat[0], 0.0, 2.0, ALU.is_ge, ALU.mult), "m_dve")
            g5 = put("dve", [g4], lambda e: e.tensor_scalar(gat[2], gat[2], -1.0, None, ALU.add), "m_dve")
            for k in (0, 3):
                put("dve", [g5], lambda e, k=k: e.tensor_tensor(
                    gat[0][:, k, :], gat[2][:, k, :], gat[1][:, k, :], ALU.mult), "m_dve")
            g6 = put("dve", [], lambda e: e.tensor_scalar(gat[0][:, 2, :], gat[0][:, 2, :], 1.0, None, ALU.add), "m_dve")
            last["gst", l] = last["scat", -1] = dma("sp", [g6], d_g[l], gat[0], f"m_gst{l}")
            last["ysfree"] = last["gst", l]
            last["mod", l] = mod_ready
            prev[:] = [mg, mg]
            return q.stream

        def later_loads():
            q.open()
            seg(1.0)
            out = {}
            out["bo"] = dma("sp", [], bos[:, :, :], bo.partition_broadcast(128), "l_bo")
            for b in range(2, NB):
                last["x", b] = dma("sp", [], X[:, NT * b:NT * b + NT, :], xv[:, NT * b:NT * b + NT, :], f"l_x{b}")
            for name, dst, src in (("f1", f1[:, :], wf1), ("f3", f3[:, :], wf3), ("f2", f2[:, :, :], wf2),
                                   ("w1", w1s[:, :], w1), ("r1", r1[:, :, :], wr1), ("r2", r2[:, :, :], wr2)):
                out[name] = dma("sp", [], dst, src, "l_" + name)
            for k in range(2):
                hv = d_h[k].rearrange("(a p) f -> p a f", p=128)
                for a in range(0, NMT, 4):
                    n = min(4, NMT - a)
                    out["h"] = dma("sp", [z5], hv[:, a:a + n, :], hs[:, 0:n, :], "c_h")
            last["hsfree"] = [out["h"]]
            return q.stream, out

        def normalise(w, i, b, x_ready, xn_free):
            seg(2.0)
            for t in range(NT):
                a = put("dve", [x_ready] if t == 0 else [], lambda e, t=t: e.bn_stats(
                    st6[:, i, t, :], X[:, NT * b + t, :]), w + "_ln")
            for t in range(NT):
                a2 = put("dve", [a], lambda e, t=t: e.bn_aggr(mv[:, i, t, :], st6[:, i, t, :]), w + "_ln")
            v = put("pool", [a2], lambda e: e.tensor_scalar(rs[:, i, 0, :], mv[:, i, :, 1], EPS, None, ALU.add), w + "_rs")
            r = put("pool", [v, c_hf], lambda e: e.tensor_tensor(rs[:, i, 1, :], rs[:, i, 0, :], half[:, :], ALU.pow), w + "_rs")
            seg(0.5)
            for t in range(NT):
                n = put("dve", [r, xn_free], lambda e, t=t: e.tensor_scalar(
                    xn[i][:, t, :], X[:, NT * b + t, :], mv[:, i, t, 0:1], rs[:, i, 1, t:t + 1],
                    ALU.subtract, ALU.mult), w + "_ln")
            return n

        def turn_modulate(w, i, l, b, ks, kc, bank, n, hT_free):
            seg(1.0)
            for t in range(NT):
                tr = put("pe", [n, c_id] + bank.free, lambda e, t=t: e.transpose(
                    bank.ap[:, 128 * t:128 * t + 128], xn[i][:, t, :], ident[:, :]), w + "_tr")
            hh = put("act", [tr, hT_free, last["mod", l]], lambda e: e.activation(
                hT[i][:, :], bank.ap[:, :], ACT.Identity, bias=mods[:, l, ks, b:b + 1],
                scale=mods[:, l, kc, b:b + 1]), w + "_hT")
            bank.free = [hh]
            return tr, hh

        N = 2 * NB

        fr = {"xn0": None, "xn1": None, "hT0": None, "hT1": None, ("sp", 0): None, ("sp", 1): None,
              "sr": None, "V": [None] * 3, "G": [None] * 2, "stackA": {}, "stackB": {}}

        def before_p(i):
            q.open()
            b = i % NB
            x_ready = last["x", b] if i < NB else last["xf", i - NB]
            last["xn", i] = normalise("p", 0, b, x_ready, fr["xn0"])
            return q.stream

        def stage_p(i):
            l, b, bank = i // NB, i % NB, banks[0]
            q.open()
            tr, hh = turn_modulate("p", 0, l, b, 0, 1, bank, last["xn", i], fr["hT0"])
            W, ws, lw = (W0, w0s, l_w0) if l == 0 else (W1, w1s, l_w1)
            src, sready = hT[0], hh
            if l == 1:
                seg(1.0)
                m = put("pe", [hh, lw] + bank.free, lambda e: e.matmul(
                    bank.ap[:, :], ws[:, W["lat"]:W["lat"] + 128], hT[0][:, :], start=True, stop=True), "p_lat")
                sready = put("act", [m], lambda e: e.activation(lat[:, :], bank.ap[:, :], ACT.Copy), "p_latc")
                bank.free = [sready]
                fr["hT0"] = m
                src = lat
            for n, (name, dd) in enumerate((("q", d_q), ("k", d_k))):
                seg(1.0)
                m = put("pe", [sready, lw] + bank.free, lambda e, name=name, src=src: e.matmul(
                    bank.ap[:, :], ws[:, W[name]:W[name] + 128], src[:, :], start=True, stop=True), "p_qk")
                s, free = sp[n], fr["sp", n]
                hi = put("act", [m, free], lambda e, s=s: e.activation(s[:, 0, :], bank.ap[:, :], ACT.Copy), "p_hi")
                rr = put("dve", [hi, m, fr["sr"], fr.get("nmr")], lambda e, s=s, n=n: e.tensor_tensor(
                    sr[:, :], bank.ap[:, :], s[:, 0, :], ALU.subtract), "p_res")
                bank.free = [hi, rr]
                mi = put("act", [rr], lambda e, s=s: e.activation(s[:, 1, :], sr[:, :], ACT.Copy), "p_mid")
                lo = put("pool", [mi], lambda e, s=s, n=n: e.tensor_tensor(
                    s[:, 2, :], sr[:, :], s[:, 1, :], ALU.subtract), "p_part")
                fr["sr"] = lo
                for k in range(3):
                    st = dma("sp", [hi, lo, last.get(("stk", i - 2, 3))],
                             dd[i % 2][k].rearrange("d (h t) -> h d t", h=H), s[:, k, :], f"p_st{name}{i % 2}")
                fr["sp", n] = st
                last["parts" + name, i] = st
            seg(1.0)
            for t in range(NT):
                m = put("pe", [sready, lw] + bank.free, lambda e, t=t, src=src: e.matmul(
                    bank.ap[:, 128 * t:128 * t + 128], src[:, 128 * t:128 * t + 128],
                    ws[:, W["v"]:W["v"] + 128], start=True, stop=True), "p_v")
            vv = put("act", [m, fr["V"][i % 3], c_v[i % 3]], lambda e: e.activation(
                VS[i % 3][:, :, :, 0:8], bank.ap[:, :].rearrange("p (t h d) -> p t h d", t=NT, h=H), ACT.Copy), "p_vc")
            bank.free = [vv]
            last["V", i] = vv
            if l == 0:
                fr["hT0"] = m
            fr["xn0"] = m
            return q.stream

        def load_stacks(i, g):
            slot = (4 * i + g) % NSLOT
            free = last.get(("sT", 4 * i + g - NSLOT))
            w = [free, last["partsq", i], last["partsk", i], c_q, c_k]
            sem, n = f"l_st{slot}", 4 * S
            kv, qv = d_k[i % 2], d_q[i % 2]
            dma("sp", w, KS[0:72, slot, :], bass.AP(
                tensor=kv.tensor, offset=kv.offset + g * n, ap=[[0, 3], [H * S, 3 * DH], [1, n]]), sem)
            for a in range(3):
                mk = dma("sp", w, QS[24 * a:24 * a + 24, slot, :], bass.AP(
                    tensor=qv.tensor, offset=qv.offset + a * DH * H * S + g * n,
                    ap=[[0, 3], [H * S, DH], [1, n]]), sem)
            last["stk", i, g] = mk

        def stage_a(i, end):
            l = i // NB
            early, late = Ring([banks[1], banks[5]]), Ring([banks[1], banks[0]])
            if i < 2:
                more = [banks[n] for n in ((1, 5, 6, 7) if i == 0 else (1, 7))]
                early, late = Ring(more), Ring(more + [banks[0]])
            pool = early
            q.open()
            for h in range(H):
                Q, K = stack(QS, i, h), stack(KS, i, h)
                for t in range(NT):
                    n = 512 if l == 0 else 128 * (t + 1)
                    seg(n / 512)
                    if sum(w for w, _ in q.stream[:-1]) >= 0.245 / end * (64.5 if l == 0 else 40.5):
                        pool = late
                    bank = pool.next()
                    m = put("pe", [last["stk", i, h // 4], c_o, c_q, c_k] + bank.free,
                            lambda e, t=t, n=n, bank=bank, Q=Q, K=K: e.matmul(
                                bank.ap[:, 0:n], Q[0:KA, 128 * t:128 * t + 128], K[0:KA, 0:n],
                                start=True, stop=(l == 0)), "a_mm")
                    if l:
                        m = put("pe", [c_ib, c_mq], lambda e, n=n, bank=bank: e.matmul(
                            bank.ap[:, n - 128:n], identb[:, :], maskq[:, :], start=False, stop=True), "a_mm")
                    r = put("dve", [m, fr.get("nm")], lambda e, h=h, t=t, n=n, bank=bank: e.tensor_reduce(
                        nm[:, 4 * h + t:4 * h + t + 1], bank.ap[:, 0:n], AX.X, ALU.max, negate=True), "a_max")
                    bank.free = [r]
            seg(0.5)
            bank = pool.next()
            tr = put("pe", [r, c_id] + bank.free, lambda e: e.transpose(
                bank.ap[0:64, 0:128], nm[:, :], ident[:, :]), "a_tr")
            fr["nm"] = tr
            hi = put("act", [tr, fr["sp", 1]], lambda e: e.activation(nmp[:, 0, :], bank.ap[0:64, 0:128], ACT.Copy), "a_hi")
            rr = put("dve", [hi, fr["sr"]], lambda e: e.tensor_tensor(
                nmr, bank.ap[0:64, 0:128], nmp[:, 0, :], ALU.subtract), "a_res")
            bank.free = [hi, rr]
            mi = put("dve", [rr], lambda e: e.tensor_copy(nmp[:, 1, :], nmr), "a_res")
            lo = put("dve", [mi], lambda e: e.tensor_tensor(nmp[:, 2, :], nmr, nmp[:, 1, :], ALU.subtract), "a_res")
            fr["nmr"] = lo
            st = dma("sp", [lo, hi], d_m[i % 2].rearrange("k r c -> r k c"), nmp, f"a_st{i % 2}")
            fr["sp", 1] = st
            for g in range(4):
                slot = (4 * i + g) % NSLOT
                last["M", i, g] = dma("sp", [st, last.get(("sT", 4 * i + g - NSLOT))],
                                      QS[96:99, slot, :].rearrange("k (r c) -> k r c", c=128),
                                      d_m[i % 2][:, 16 * g:16 * g + 16, :], f"a_ld{slot}")
            return q.stream

        ering = Ring(list(range(NE_)))
        efree = [None] * NE_

        def stage_b(i):
            l, pool, pv = i // NB, Ring([banks[2], banks[3]] + [banks[1]] * (i == N - 1)), banks[4]
            V = VS[i % 3]
            scale = SC1 if l else SC0
            q.open()
            lag, ust = [], []

            def attend(g, j, q0, slots):
                for a, (s, ex) in enumerate(slots):
                    m = put("pe", [ex, last["V", i], c_p] + (pv.free if j == 0 else []),
                            lambda e, a=a, s=s, j=j, h=4 * g + a: e.matmul(
                                pv.ap[32 * a:32 * a + 16, q0:512], V[:, j, h, :], ES[s][:, 0:512 - q0],
                                start=(j == 0), stop=(j == NT - 1), skip_group_check=True), "b_pv")
                    efree[s] = m
                if j == NT - 1:
                    u = put("act", [m, fr.get(("U", g % 2))], lambda e: e.activation(US[g % 2][:, :], pv.ap[:, :], ACT.Copy), "b_u")
                    pv.free = [u]
                    for a in range(4):
                        last["U", i] = fr["U", g % 2] = dma("sp", [u], d_u[i % 2][g, a], US[g % 2][32 * a:32 * a + 16, :],
                                                            f"b_stu{i % 2}{g}")
                    ust.append(last["U", i])
                if (g, j) == (3, NT - 1):
                    fr["V"][i % 3] = m

            for g in range(4):
                for j in range(NT):
                    q0 = 0 if l == 0 else 128 * j
                    slots = []
                    for a in range(4):
                        h = 4 * g + a
                        Q, K = stack(QS, i, h), stack(KS, i, h)
                        seg((512 - q0) / 512)
                        bank = pool.next()
                        m = put("pe", [last["M", i, g]] + bank.free, lambda e, j=j, bank=bank, q0=q0, Q=Q, K=K: e.matmul(
                            bank.ap[:, 0:512 - q0], K[0:KB, 128 * j:128 * j + 128], Q[0:KB, q0:512],
                            start=True, stop=(l == 0)), "b_mm")
                        last["sT", 4 * i + g] = m
                        if l:
                            m = put("pe", [], lambda e, bank=bank: e.matmul(
                                bank.ap[:, 0:128], identb[:, :], maskk[:, :], start=False, stop=True), "b_mm")
                        s = ering.next()
                        ex = put("act", [m, efree[s]], lambda e, s=s, bank=bank, q0=q0: e.activation(
                            ES[s][:, 0:512 - q0], bank.ap[:, 0:512 - q0], ACT.Exp, scale=scale), "b_exp")
                        bank.free = [ex]
                        slots.append((s, ex))
                    nxt = 4 * i + g + NSLOT
                    if j == NT - 1 and nxt < 8 * NB:
                        load_stacks(nxt // 4, nxt % 4)
                    if lag:
                        seg(1.0 if i < 4 else 2.0)
                        attend(*lag.pop())
                    lag.append((g, j, q0, slots))
            seg(1.0)
            attend(*lag.pop())
            seg(0.1)
            uv = d_u[i % 2].rearrange("g a r t -> (g a) r t")
            ld = dma("sp", ust + [fr.get("DC")], DC[:, 0, :], uv[:, 8, :].rearrange("h (b c) -> h b c", b=8), "b_ldd")
            last["OT", i] = dma("sp", ust + [fr.get("OT")], OT[:, :], uv[:, 0:8, :], "b_ldo")
            last["DC", i] = ld
            return q.stream

        def stage_t(i):
            l, b, bank = i // NB, i % NB, banks[7]
            W, ws, lw = (W0, w0s, l_w0) if l == 0 else (W1, w1s, l_w1)
            q.open()
            seg(1.0)
            last["G", i] = dma("sp", [fr["G"][i % 2], last["gst", l]], GT[i % 2][:, :, :],
                               d_g[l, b].partition_broadcast(128), f"t_g{i % 2}")
            rc = put("dve", [last["DC", i], fr.get("DC2")], lambda e: e.reciprocal(DC[:, 1, :], DC[:, 0, :]), "b_rc")
            fr["DC"] = rc
            s2 = dma("sp", [rc], d_r[i % 2].rearrange("h (b c) -> (h b) c", b=8), DC[:, 1, :], "b_str")
            fr["DC2"] = s2
            rv = d_r[i % 2]
            last["DR", i] = dma("sp", [s2, fr.get("DR")], DR[:, :], bass.AP(
                tensor=rv.tensor, offset=rv.offset, ap=[[S, H], [0, DH], [1, S]]), "b_ldr")
            seg(0.2)
            o = put("dve", [last["OT", i], last["DR", i]], lambda e: e.tensor_tensor(
                OT[:, :], OT[:, :], DR[:, :], ALU.mult), "t_o")
            fr["DR"] = o
            seg(0.5)
            for t in range(NT):
                m = put("pe", [o, lw] + bank.free, lambda e, t=t: e.matmul(
                    bank.ap[:, 128 * t:128 * t + 128], OT[:, 128 * t:128 * t + 128],
                    ws[:, W["o"]:W["o"] + 128], start=True, stop=True), "t_mm")
            fr["OT"] = m
            bb = bos[:, l:l + 1, :].broadcast_to([128, NT, 128])
            a = put("dve", [m, l_bo, ytf[0]], lambda e: e.tensor_tensor(
                pt[:, :, :], bank.ap[:, :].rearrange("p (t f) -> p t f", t=NT), bb, ALU.add), "t_b")
            bank.free = [a]
            gg = GT[i % 2][:, 0:1, :].broadcast_to([128, NT, 128])
            eng, tag = ("dve", "t_xd") if l == 0 or i == NB + 2 or i >= N - 3 else ("pool", "t_xp")
            g = put(eng, [a, last["G", i]], lambda e: e.tensor_tensor(pt[:, :, :], pt[:, :, :], gg, ALU.mult), tag)
            xs = X[:, NT * b:NT * b + NT, :]
            last["xt", i] = put(eng, [g], lambda e: e.tensor_tensor(xs, xs, pt[:, :, :], ALU.add), tag)
            return q.stream

        up_a, up_b, low = banks[5], banks[6], banks[7]
        hb = Places(NHD, None)
        tfree, ytf = [None], [None]

        def both(one, two):
            q.open()
            keyed = [((n + 0.5) / len(one), 0, f) for n, f in enumerate(one)]
            keyed += [((n + 0.5) / len(two), 1, f) for n, f in enumerate(two)]
            for _, _, f in sorted(keyed, key=lambda x: x[:2]):
                f()
            return q.stream

        def top_two(i, c, pool):
            l, b = i // NB, i % NB
            W, ws, lw = (W0, w0s, l_w0) if l == 0 else (W1, w1s, l_w1)

            def norm():
                n = normalise("f", 1, b, last["xt", i], fr.get("ya"))
                c["tr"], c["hh"] = turn_modulate("f", 1, l, b, 3, 4, pool.next(), n, fr["hT1"])

            def logits():
                seg(2.0)
                bank = pool.next()
                for t in range(NT):
                    m = put("pe", [c["hh"], lw] + bank.free, lambda e, t=t: e.matmul(
                        bank.ap[:, E * t:E * t + E], hT[1][:, 128 * t:128 * t + 128], ws[:, W["g"]:W["g"] + E],
                        start=True, stop=True), "f_g")
                c["hT"] = m
                c0 = put("dve", [m], lambda e: e.tensor_copy(lg[:, 0, :, :], bank.ap[:, 0:NT * E].rearrange(
                    "p (t e) -> p t e", t=NT)), "f_r")
                bank.free = [c0]
                c1 = put("dve", [c0], lambda e: e.tensor_reduce(sm[:, 0, :], lg[:, 0, :, :], AX.X, ALU.max), "f_r")
                c2 = put("dve", [c1], lambda e: e.tensor_tensor(
                    lg[:, 1, :, :], lg[:, 0, :, :], sm[:, 0, :].unsqueeze(2).broadcast_to([128, NT, E]),
                    ALU.subtract), "f_r")
                c["ex"] = put("act", [c2], lambda e: e.activation(lg[:, 2, :, :], lg[:, 1, :, :], ACT.Exp), "f_e")

            def probs():
                seg(0.3)
                c3 = put("dve", [c["ex"]], lambda e: e.tensor_reduce(sm[:, 1, :], lg[:, 2, :, :], AX.X, ALU.add), "f_r")
                c4 = put("dve", [c3], lambda e: e.reciprocal(sm[:, 2, :], sm[:, 1, :]), "f_r")
                c5 = put("dve", [c4], lambda e: e.tensor_tensor(
                    lg[:, 3, :, :], lg[:, 2, :, :], sm[:, 2, :].unsqueeze(2).broadcast_to([128, NT, E]),
                    ALU.mult), "f_r")
                for t in range(NT):
                    c["m8"] = put("dve", [c5], lambda e, t=t: e.max(m8[:, t, :], lg[:, 3, t, :]), "f_r")

            def indices():
                seg(0.3)
                for t in range(NT):
                    c7 = put("dve", [c["m8"]], lambda e, t=t: e.max_index(i8[:, t, :], m8[:, t, :], lg[:, 3, t, :]), "f_r")
                c8 = put("dve", [c7], lambda e: e.tensor_copy(if8[:, :, :], i8[:, :, :]), "f_r")
                io = iota8[:, :].unsqueeze(1).broadcast_to([128, NT, E])
                for k in range(2):
                    c["oh"] = put("dve", [c8, c_io], lambda e, k=k: e.tensor_tensor(
                        lg[:, 4 + k, :, :], io, if8[:, :, k:k + 1].broadcast_to([128, NT, E]), ALU.is_equal), "f_r")

            return [norm, logits, probs, indices]

        def route(i):
            c, p, o = {}, i // 2, NT * (i % 2)
            pool = Ring([up_a, up_b])
            X_ = X[:, NT * (i % NB):NT * (i % NB) + NT, :]

            def modulated():
                seg(0.1)
                g = GT[i % 2]
                a = put("pool", [c["tr"], last["G", i], last.get(("scat", p - 1))], lambda e: e.tensor_tensor(
                    hx[i % 2][:, :, :], xn[1], g[:, 2:3, :].broadcast_to([128, NT, 128]), ALU.mult), "r_hx")
                last["hx", i] = put("pool", [a], lambda e: e.tensor_tensor(
                    hx[i % 2][:, :, :], hx[i % 2][:, :, :], g[:, 1:2, :].broadcast_to([128, NT, 128]), ALU.add), "r_hx")
                fr["ya"] = a

            def keep():
                seg(0.1)
                for k in range(2):
                    put("dve", [c["oh"]], lambda e, k=k: e.tensor_copy(ohs[:, k, o:o + NT, :], lg[:, 4 + k, :, :]), "r_d")
                c["keep"] = put("dve", [last.get(("comb", p - 2))], lambda e: e.tensor_scalar(
                    wts[p % 2][:, o:o + NT, :], m8[:, :, 0:2], 0.5, None, ALU.mult), "r_d")

            def shared(n):
                def f():
                    r0 = E * 352 + 128 * n
                    seg(2.0)
                    ma = put("pe", [c["hh"], l_f1] + up_a.free, lambda e: e.matmul(
                        up_a.ap[:, :], f1[:, r0:r0 + 128], hT[1][:, :], start=True, stop=True), "f_up")
                    mb = put("pe", [l_f3] + up_b.free, lambda e: e.matmul(
                        up_b.ap[:, :], f3[:, r0:r0 + 128], hT[1][:, :], start=True, stop=True), "f_up")
                    s, sfree = hb.take()
                    th = put("act", [ma, tfree[0]], lambda e: e.activation(tt[0][:, :], up_a.ap[:, :], ACT.Tanh, scale=0.5), "f_th")
                    u = put("dve", [th, ma, sfree], lambda e: e.scalar_tensor_tensor(
                        out=hd[s][:, :], in0=tt[0][:, :], scalar=1.0, in1=up_a.ap[:, :], op0=ALU.add, op1=ALU.mult), "f_u")
                    hm = put("dve", [u, mb], lambda e: e.tensor_tensor(
                        hd[s][:, :], up_b.ap[:, :], hd[s][:, :], ALU.mult), "f_u")
                    tfree[0] = u
                    up_a.free, up_b.free = [u], [hm]
                    fr["hT1"] = mb
                    c["sh", n] = (s, hm)
                return f

            def shared_down():
                for t in range(NT):
                    seg(0.5)
                    for n in range(2):
                        s, ready = c["sh", n]
                        m = put("pe", [ready, l_f2] + low.free, lambda e, t=t, n=n, s=s: e.matmul(
                            low.ap[:, 128 * t:128 * t + 128], hd[s][:, 128 * t:128 * t + 128], f2[:, 3 * E + n, :],
                            start=(n == 0), stop=(n == 1)), "f_dn")
                for n in range(2):
                    hb.give(c["sh", n][0], m)
                d = put("dve", [m, ytf[0]], lambda e: e.tensor_scalar(
                    yt[0][:, :, :], low.ap[:, :].rearrange("p (t f) -> p t f", t=NT), 0.5, None, ALU.mult), "f_y")
                low.free = [d]
                g = put("pool", [d, last["G", i]], lambda e: e.tensor_tensor(
                    yt[0][:, :, :], yt[0][:, :, :], GT[i % 2][:, 3:4, :].broadcast_to([128, NT, 128]), ALU.mult), "f_x")
                x = put("pool", [g], lambda e: e.tensor_tensor(X_, X_, yt[0][:, :, :], ALU.add), "f_x")
                ytf[0] = x
                fr["G"][i % 2] = x
                last["xr", i] = x

            def ranks():
                seg(0.3)
                s = put("dve", [c["keep"], fr.get("ohb")], lambda e: e.tensor_tensor(
                    ohb[:, :].rearrange("p (e t) -> p t e", e=E), ohs[:, 0, :, :], ohs[:, 1, :, :], ALU.add), "r_d")
                bank = pool.next()
                put("pe", [s, c_rt] + bank.free, lambda e: e.matmul(
                    bank.ap[:, 0:64], before[:, :], ohb[:, :], start=True, stop=True), "r_mm")
                m = put("pe", [], lambda e: e.matmul(
                    bank.ap[:, 64:128], onesb[:, :], ohb[:, :], start=True, stop=True), "r_mm")
                fr["ohb"] = m
                cp = put("dve", [m], lambda e: e.tensor_copy(rt[:, 0:2, :], bank.ap[:, 0:128].rearrange(
                    "p (a b) -> p a b", a=2)), "r_d")
                bank.free = [cp]
                sc = put("dve", [cp], lambda e: e.tensor_tensor_scan(
                    rt[:, 2, :], seg8[:, :, :].rearrange("p e t -> p (e t)"), rt[:, 1, :], 0.0, ALU.mult, ALU.add), "r_d")
                put("dve", [sc], lambda e: e.tensor_tensor(rt[:, 3, :], rt[:, 2, :], rt[:, 1, :], ALU.subtract), "r_d")
                n_ = rt[:, 2, :].rearrange("p (e t) -> p e t", e=E)[:, :, 7:8].broadcast_to([128, E, 8])
                c["gt"] = put("dve", [sc], lambda e: e.tensor_tensor(
                    rj[:, 0:8, :], n_, k128[:, :].unsqueeze(1).broadcast_to([128, E, 8]), ALU.is_gt), "r_d")

            def places():
                seg(0.3)
                put("dve", [c["gt"]], lambda e: e.tensor_tensor(rt[:, 3, :], rt[:, 3, :], rt[:, 0, :], ALU.add), "r_d")
                a = put("dve", [c["gt"]], lambda e: e.tensor_reduce(re_[:, 0, :], rj[:, 0:8, :], AX.X, ALU.add), "r_d")
                b_ = put("dve", [a], lambda e: e.tensor_tensor_scan(
                    re_[:, 1, :], one8[:, :], re_[:, 0, :], 0.0, ALU.mult, ALU.add), "r_d")
                d = put("dve", [b_], lambda e: e.tensor_tensor(re_[:, 2, :], re_[:, 1, :], re_[:, 0, :], ALU.subtract), "r_d")
                f = put("dve", [d], lambda e: e.tensor_scalar(re_[:, 3, :], re_[:, 2, :], 128.0, None, ALU.mult), "r_d")
                r_ = rt[:, 3, :].rearrange("p (e t) -> p e t", e=E)
                g = put("dve", [f], lambda e: e.tensor_tensor(
                    rt[:, 4, :].rearrange("p (e t) -> p e t", e=E), r_, re_[:, 3, :].unsqueeze(2).broadcast_to([128, E, 8]),
                    ALU.add), "r_d")
                sv = rt[:, 4, :].rearrange("p (e t) -> p t e", e=E)
                for k in range(2):
                    h = put("dve", [g], lambda e, k=k: e.tensor_tensor(ohs[:, k, :, :], ohs[:, k, :, :], sv, ALU.mult), "r_d")
                u = put("dve", [h], lambda e: e.tensor_reduce(
                    rt[:, 5, 0:16].rearrange("p (k t) -> p k t", k=2), ohs[:, :, :, :], AX.X, ALU.add), "r_d")
                c["pos"] = put("dve", [u, last.get(("comb", p - 2))], lambda e: e.tensor_copy(
                    pos[p % 2][:, :, :], rt[:, 5, 0:16].rearrange("p (k t) -> p k t", k=2)), "r_d")
                c["inc"] = b_

            def tiles():
                seg(0.3)
                a = put("dve", [c["inc"]], lambda e: e.tensor_tensor(
                    rj[:, :, :], i24[:, :].unsqueeze(2).broadcast_to([128, 24, E]),
                    re_[:, 1, :].unsqueeze(1).broadcast_to([128, 24, E]), ALU.is_ge), "r_d")
                b_ = put("dve", [a], lambda e: e.tensor_reduce(te[:, :], rj[:, :, :], AX.X, ALU.add), "r_d")
                for k, n in enumerate((352.0, 384.0)):
                    last["tex", p] = put("dve", [b_, last.get(("regs", p - 2))], lambda e, k=k, n=n: e.tensor_scalar(
                        tex[p % 2][:, k, :], te[:, :], float(E - 1), n, ALU.min, ALU.mult), "r_d")

            def scatter(t8):
                def f():
                    seg(0.1)
                    for k in range(2):
                        last["scat", p] = put("pool", [c["pos"], last["hx", i], last["hx", i - 1], c_h, last.get(("loaded", p - 2))],
                            lambda e, k=k: e.indirect_dma_start(
                                out=d_h[p % 2][:, :], out_offset=bass.IndirectOffsetOnAxis(ap=pos[p % 2][:, k, t8:t8 + 1], axis=0),
                                in_=hx[t8 // NT][:, t8 % NT, :], in_offset=None, bounds_check=NMT * 128 - 1), "r_sc", 16)
                return f

            norm, logits, probs, indices = top_two(i, c, pool)
            out = [norm, modulated, logits, probs, shared(0), indices, keep]
            if i % 2:
                out += [ranks, places, tiles] + [scatter(t) for t in range(4)]
            out += [shared(1)]
            if i % 2:
                out += [scatter(t) for t in range(4, 8)]
            return out + [shared_down]

        regs = {}

        ahead = {}

        def load_rows(p, j, n):
            hv = d_h[p % 2].rearrange("(a p) f -> p a f", p=128)
            last["loaded", p] = dma("sp", [last["scat", p]] + last["hsfree"], hs[:, 0:n, :], hv[:, j:j + n, :], "x_ld")
            return last["loaded", p]

        def first_rows(p):
            q.open()
            seg(0.1)
            ahead[0] = load_rows(p, 0, 4)
            return q.stream

        def moe(p, half):
            lo, hi = (0, 12) if half == 0 else (12, NMT)
            c = {}
            yv = d_y[p % 2].rearrange("(a p) f -> p a f", p=128)

            def load(j):
                c["ld", j] = load_rows(p, j, min(4, hi - j))

            def start():
                seg(0.1)

                def read(e):
                    if not regs:
                        for k in range(2):
                            regs[k] = [e.alloc_register(f"row{k}_{n}") for n in range(12)]
                    for k in range(2):
                        e.reg_load(regs[k], tex[p % 2][0:1, k, 12 * half:12 * half + 12])
                    return e.nop()

                last["regs", p] = put("pe", [last["tex", p]], read, "x_rg")
                c["ld", lo] = ahead[half]

            def turn_rows(j):
                def f():
                    n, T_ = min(4, hi - j), hsT[(j // 4) % 2]
                    seg(0.25 * n)
                    for t in range(n):
                        m = put("pe", [c["ld", j], c_id] + low.free, lambda e, t=t: e.transpose(
                            low.ap[:, 128 * t:128 * t + 128], hs[:, t, :], ident[:, :]), "x_tr")
                    last["hsfree"] = [m]
                    cp = put("act", [m, fr.get(("hsT", (j // 4) % 2))], lambda e: e.activation(
                        T_[:, 0:128 * n], low.ap[:, 0:128 * n], ACT.Copy), "x_cp")
                    low.free = [cp]
                    c["T", j // 4] = cp
                    if j + 4 < hi:
                        load(j + 4)
                    elif half == 0:
                        ahead[1] = load_rows(p, hi, 4)
                return f

            def up(j):
                def f():
                    seg(1.8)
                    T_, a0, n = hsT[(j // 4) % 2], 128 * (j % 4), j - lo

                    def mm(e, bank, w):
                        v = e.snap(regs[0][n], min_val=0, max_val=7 * 352)
                        return e.matmul(bank.ap[:, 0:352], T_[:, a0:a0 + 128], w[:, bass.ds(v, 352)], start=True, stop=True)

                    ma = put("pe", [c["T", j // 4], l_f1] + up_a.free, lambda e: mm(e, up_a, f1), "x_up")
                    mb = put("pe", [l_f3] + up_b.free, lambda e: mm(e, up_b, f3), "x_up")
                    fr["hsT", (j // 4) % 2] = mb
                    dn = down(j - 1) if j > lo else None
                    s, sfree = hb.take()
                    th = put("act", [ma, tfree[0]], lambda e: e.activation(
                        tt[0][:, 0:352], up_a.ap[:, 0:352], ACT.Tanh, scale=0.5), "x_th")
                    u = put("dve", [th, ma, sfree], lambda e: e.scalar_tensor_tensor(
                        out=hd[s][:, 0:352], in0=tt[0][:, 0:352], scalar=1.0, in1=up_a.ap[:, 0:352],
                        op0=ALU.add, op1=ALU.mult), "x_u")
                    hm = put("dve", [u, mb, dn], lambda e: e.tensor_tensor(
                        hd[s][:, 0:352], up_b.ap[:, 0:352], hd[s][:, 0:352], ALU.mult), "x_u")
                    tfree[0] = u
                    up_a.free, up_b.free = [u], [hm]
                    c["hid", j] = (s, hm)
                    if dn:
                        result(j - 1, dn)
                return f

            def turn(j):
                def f():
                    seg(0.65)
                    s, ready = c["hid", j]
                    for n, w in enumerate((128, 128, 96)):
                        m = put("pe", [ready] + low.free, lambda e, n=n, w=w: e.transpose(
                            low.ap[0:w, 128 * n:128 * n + 128], hd[s][:, 128 * n:128 * n + w], ident[:, :]), "x_tu")
                    hb.give(s, m)
                    s2, sfree = hb.take()
                    cp = put("act", [m, sfree], lambda e: e.activation(
                        hd[s2][:, 0:384], low.ap[:, 0:384], ACT.Copy), "x_ht")
                    low.free = [cp]
                    c["hT", j] = (s2, cp)
                return f

            def down(j):
                s, ready = c["hT", j]
                for n, w in enumerate((128, 128, 96)):
                    def mm(e, n=n, w=w):
                        v = e.snap(regs[1][j - lo], min_val=0, max_val=7 * 384)
                        f2v = f2[:, :, :].rearrange("p a b -> p (a b)")
                        return e.matmul(up_b.ap[:, 352:480], hd[s][0:w, 128 * n:128 * n + 128],
                                        f2v[0:w, bass.ds(v + 128 * n, 128)], start=(n == 0), stop=(n == 2))
                    m = put("pe", [ready, l_f2], mm, "x_dn")
                hb.give(s, m)
                return m

            def result(j, dn):
                k, n = (j - lo) % 4, min(4, hi - (j - (j - lo) % 4))
                d = put("dve", [dn, last.get("ysfree") if k == 0 else None], lambda e: e.tensor_copy(
                    ys[:, k, :], up_b.ap[:, 352:480]), "x_y")
                up_b.free = up_b.free + [d]
                if k == n - 1:
                    j0 = j - k
                    last["ysfree"] = dma("sp", [d, last.get(("comb", p - 2))], yv[:, j0:j0 + n, :], ys[:, 0:n, :], "x_st")
                    last["ys", p] = last["ysfree"]

            def final():
                seg(0.65)
                put("pe", up_b.free, lambda e: e.nop())
                result(hi - 1, down(hi - 1))

            out = [start]
            for j in range(lo, hi):
                if j % 4 == 0:
                    out.append(turn_rows(j))
                if j > lo:
                    out.append(turn(j - 1))
                out.append(up(j))
            return out + [turn(hi - 1), final]

        def gather(p):
            q.open()
            gs, ix = [None] * 4, 0
            for i in (2 * p, 2 * p + 1):
                b = i % NB
                seg(0.1)
                gcl = dma("sp", [fr.get("GC")], GC[:, :], d_g[0, b, 3].partition_broadcast(128), "g_gc")
                for t in range(NT):
                    seg(1.0)
                    t8, mk = NT * (i % 2) + t, []
                    for k in range(2):
                        n = ix % 4
                        ix += 1
                        mk.append((n, put("pool", [last["ys", p], fr.get(("gr", n))], lambda e, n=n, k=k, t8=t8: e.indirect_dma_start(
                            out=gr[n][:, :], out_offset=None, in_=d_y[p % 2][:, :],
                            in_offset=bass.IndirectOffsetOnAxis(ap=pos[p % 2][:, k, t8:t8 + 1], axis=0),
                            bounds_check=NMT * 128 - 1), f"g_ga{n}", 16)))
                    last["gath", p] = mk[1][1]
                    (n0, m0), (n1, m1) = mk
                    c["later"] = c.get("later", []) + [(t, t8, n0, m0, n1, m1)]
                    if len(c["later"]) == 2:
                        weigh(*c["later"].pop(0), p)
                weigh(*c["later"].pop(0), p)
                seg(0.5)
                a = put("pool", [last["wd"], gcl], lambda e: e.tensor_tensor(
                    cv[:, :, :], cv[:, :, :], GC[:, :].unsqueeze(1).broadcast_to([128, NT, 128]), ALU.mult), "g_x")
                fr["GC"] = a
                xs = X[:, NT * b:NT * b + NT, :]
                x = put("pool", [a, last["xr", i]], lambda e, xs=xs: e.tensor_tensor(xs, xs, cv[:, :, :], ALU.add), "g_x")
                fr["cv"] = x
                last["xf", i] = x
            last["comb", p] = last["wd"]
            return q.stream

        c = {}

        def weigh(t, t8, n0, m0, n1, m1, p):
            a = put("dve", [m0, fr.get("cv")], lambda e: e.tensor_scalar(
                cv[:, t, :], gr[n0][:, :], wts[p % 2][:, t8, 0:1], None, ALU.mult), "g_w")
            d = put("dve", [a, m1], lambda e: e.scalar_tensor_tensor(
                out=cv[:, t, :], in0=gr[n1][:, :], scalar=wts[p % 2][:, t8, 1:2], in1=cv[:, t, :],
                op0=ALU.mult, op1=ALU.add), "g_w")
            fr["gr", n0], fr["gr", n1] = a, d
            last["wd"] = d

        def dense(i):
            l, b = 1, i % NB
            c, pool = {}, Ring([up_a])
            ups = Ring([up_a] + [banks[0]] * (i >= N - 2))
            lows = Ring([low] + [up_b] * (i >= NB + 2) + [banks[1]] * (i == N - 1))
            norm, logits, probs, indices = top_two(i, c, pool)
            pend = []

            def comb():
                seg(0.1)
                for k in range(2):
                    a = put("dve", [c["oh"]], lambda e, k=k: e.tensor_tensor(
                        lg[:, 4 + k, :, :], lg[:, 4 + k, :, :], m8[:, :, k:k + 1].broadcast_to([128, NT, E]), ALU.mult), "f_r")
                c["comb"] = put("dve", [a], lambda e: e.tensor_tensor(
                    lg[:, 0, :, :], lg[:, 4, :, :], lg[:, 5, :, :], ALU.add), "f_r")

            def expert(k):
                def f():
                    seg(1.0)
                    up = ups.next()
                    ma = put("pe", [c["hh"], l_r1] + up.free, lambda e: e.matmul(
                        up.ap[:, :], r1[:, k, :], hT[1][:, :], start=True, stop=True), "f_up")
                    fr["hT1"] = ma
                    s, sfree = hb.take()
                    re = put("act", [ma, tfree[0]], lambda e: e.activation(tt[0][:, :], up.ap[:, :], ACT.Relu), "f_th")
                    up.free = [re]
                    hm = put("dve", [re, sfree], lambda e: e.tensor_tensor(
                        hd[s][:, :], tt[0][:, :], tt[0][:, :], ALU.mult), "f_u")
                    tfree[0] = hm
                    pend.append((k, s, hm))
                    if len(pend) == 2:
                        down(*pend.pop(0))
                return f

            def down(k, s, ready):
                low = lows.next()
                for t in range(NT):
                    m = put("pe", [ready, l_r2] + low.free, lambda e, t=t: e.matmul(
                        low.ap[:, 128 * t:128 * t + 128], hd[s][:, 128 * t:128 * t + 128], r2[:, k, :],
                        start=True, stop=True), "f_dn")
                    seg(0.25)
                hb.give(s, m)
                yv = low.ap[:, :].rearrange("p (t f) -> p t f", t=NT)
                cb = lg[:, 0, :, k].unsqueeze(2).broadcast_to([128, NT, 128])
                if k == 0:
                    d = put("dve", [m, c["comb"], fr.get("ya")], lambda e: e.tensor_tensor(ya[:, :, :], yv, cb, ALU.mult), "f_y")
                    c["ya"] = d
                else:
                    d = put("dve", [m, ytf[0]], lambda e: e.tensor_tensor(yt[0][:, :, :], yv, cb, ALU.mult), "f_y")
                    eng, tag = ("dve", "f_yd") if (i, k) == (N - 1, E - 1) else ("pool", "f_ya")
                    c["ya"] = ytf[0] = put(eng, [d, c["ya"]], lambda e: e.tensor_tensor(
                        ya[:, :, :], ya[:, :, :], yt[0][:, :, :], ALU.add), tag)
                low.free = [d]

            def end():
                down(*pend.pop(0))
                gg = GT[i % 2][:, 3:4, :].broadcast_to([128, NT, 128])
                eng, tag = ("dve", "f_xd") if i == N - 1 else ("pool", "f_xp")
                g = put(eng, [c["ya"], last["G", i]], lambda e: e.tensor_tensor(ya[:, :, :], ya[:, :, :], gg, ALU.mult), tag)
                xs = X[:, NT * b:NT * b + NT, :]
                fx = put(eng, [g], lambda e: e.tensor_tensor(xs, xs, ya[:, :, :], ALU.add), tag)
                fr["ya"] = fx
                fr["G"][i % 2] = fx
                ov = out.rearrange("b (t p) d -> p (b t) d", p=128)
                last["out", b] = dma("pool", [fx], ov[:, NT * b:NT * b + NT, :], xs, "f_out")

            return [norm, logits, probs, expert(0), indices, comb] + [expert(k) for k in range(1, E)] + [end]

        order = merge([(setup, 0, 1), (before_p(0), 1, 2), (modulation(0, l_c, l_wm), 3, 4)])
        for s in range(N + 3):
            parts = []
            if s < N:
                parts.append((stage_p(s), 0.0, 0.24))
            if 0 <= s - 2 < N:
                parts.append((stage_b(s - 2), 0.04, 1.0))
            if 0 <= s - 1 < N:
                end = 0.9 if s - 1 < NB else 0.8
                parts.append((stage_a(s - 1, end), 0.0, end))
            if 0 <= s - 3 < N:
                parts.append((stage_t(s - 3), 0.1, 0.25 if s - 3 < NB else 0.28 if s < N else 0.4))
            p, part = (s - 5) // 2, (s - 5) % 2
            if part == 0 and 0 <= p < NB // 2:
                parts.append((first_rows(p), 0.03, 0.04))
            rows = moe(p, part) if 0 <= p < NB // 2 else []
            own = (route(s - 3) if s - 3 < NB else dense(s - 3)) if 0 <= s - 3 < N else []
            if rows or own:
                parts.append((both(own, rows), 0.26 if s - 3 < NB else 0.3 if s < N else 0.42, 1.0))
            p = (s - 7) // 2
            if (s - 7) % 2 == 0 and 0 <= p < NB // 2:
                parts.append((gather(p), 0.25, 0.85))
            if s == 2:
                parts.append((modulation(1, None, None), 0.3, 0.8))
            if s + 1 < N:
                parts.append((before_p(s + 1), 0.92, 0.97))
            order += merge(parts)
            if s < 2:
                q.open()
                seg(0)
                for g in range(4 if s == 0 else 2):
                    load_stacks(s, g)
                order += merge([(q.stream, 0, 1)])
            if s == 0:
                rest, l_ = later_loads()
                l_bo, l_f1, l_f3, l_f2, l_w1, l_r1, l_r2, c_h = (
                    l_[n] for n in ("bo", "f1", "f3", "f2", "w1", "r1", "r2", "h"))
                order += merge([(rest, 0, 1)])
        q.open()
        seg(0)
        order += [("sp", [last["out", NB - 1]], None, None, 0)]

        issued = {}
        for who, waits, fn, sem, by in order:
            assert all(issued.get(w.sem, 0) >= w.value for w in waits), (who, sem)
            issued[sem] = issued.get(sem, 0) + by
        sems = {name: ctx.enter_context(nc.semaphore(name)) for name in q.count}
        block = ctx.enter_context(nc.Block())

        def issue(name, eng):
            seen = {}
            for who, waits, fn, sem, by in order:
                if who != name:
                    continue
                for w in waits:
                    if seen.get(w.sem, 0) < w.value:
                        eng.wait_ge(sems[w.sem], w.value)
                        seen[w.sem] = w.value
                if fn is None:
                    continue
                ins = fn(eng)
                if sem is not None:
                    ins.then_inc(sems[sem], by)

        @block.tensor
        def _(eng):
            issue("pe", eng)

        @block.vector
        def _(eng):
            issue("dve", eng)

        @block.scalar
        def _(eng):
            issue("act", eng)

        @block.gpsimd
        def _(eng):
            issue("pool", eng)

        @block.sync
        def _(eng):
            issue("sp", eng)


def kernel(**inputs):
    import numpy as _np
    import concourse.bacc as _bacc
    from concourse import mybir as _mybir
    from concourse.bass_utils import run_bass_kernel_spmd as _run

    x = {k: _np.asarray(v) for k, v in inputs.items()}
    f = x["L0_attn_x"].dtype

    def cols(w, n):
        out = _np.zeros((128, n), w.dtype)
        out[:w.shape[0], :w.shape[1]] = w
        return out

    wqkv = x["L0_attn_w_qkv"]
    w0 = _np.concatenate([wqkv[0:128].T, wqkv[128:256].T, wqkv[256:384].T,
                          x["L0_attn_w_out"].T, x["L0_ffn_gate_w"].T], 1)
    lat = cols(_np.concatenate([x["L1_attn_wq_lat"], x["L1_attn_wk_lat"], x["L1_attn_wv_lat"]], 1), 128)
    heads = []
    for n, name in enumerate(("q", "k", "v")):
        h = _np.zeros((128, 128), f)
        h[32 * n:32 * n + 32] = x[f"L1_attn_w{name}_heads"]
        heads.append(h)
    w1 = _np.concatenate([lat] + heads + [x["L1_attn_w_proj"], x["L1_ffn_Wr"]], 1)

    def up(w, s):
        out = _np.zeros((128, 8 * 352 + 256), w.dtype)
        out[:, :8 * 352] = w.transpose(1, 0, 2).reshape(128, 8 * 352)
        out[:, 8 * 352:8 * 352 + 192] = s
        return out

    def down(w, s):
        out = _np.zeros((26, 128, 128), w.dtype)
        a = _np.zeros((8, 384, 128), w.dtype)
        a[:, :352] = w
        out[:24] = a.reshape(24, 128, 128)
        b = _np.zeros((256, 128), w.dtype)
        b[:192] = s
        out[24:] = b.reshape(2, 128, 128)
        return out.transpose(1, 0, 2)

    args = {
        "xin": x["L0_attn_x"],
        "cT": _np.stack([x["L0_c"].T, x["L1_c"].T]),
        "wm": _np.stack([x["L0_wmod"], x["L1_wmod"]]),
        "w0": w0,
        "wf1": up(x["L0_ffn_w1"], x["L0_ffn_sw1"]),
        "wf3": up(x["L0_ffn_w3"], x["L0_ffn_sw3"]),
        "wf2": down(x["L0_ffn_w2"], x["L0_ffn_sw2"]),
        "w1": w1,
        "wr1": x["L1_ffn_W1"].transpose(1, 0, 2),
        "wr2": x["L1_ffn_W2"].transpose(1, 0, 2),
        "bo": _np.stack([x["L0_attn_b_out"], x["L1_attn_b_proj"]]),
    }
    nc = _bacc.Bacc("TRN2", target_bir_lowering=False, num_devices=1)
    arrays, aps = {}, []
    for name, a in args.items():
        a = _np.ascontiguousarray(a)
        arrays[name] = a
        aps.append(nc.dram_tensor(name, a.shape, _mybir.dt.from_np(a.dtype), kind="ExternalInput").ap())
    o = nc.dram_tensor("y", (8, 512, 128), _mybir.dt.float32, kind="ExternalOutput").ap()
    program(nc, *aps, o)
    r = _run(nc, [arrays], core_ids=[0])
    return r.results[0]["y"]
```
